# Optimizing a Trainium2 kernel written in Bass

```python
import numpy as np
import jax
import jax.numpy as jnp

def _softmax(x, axis=-1):
    return jax.nn.softmax(x, axis=axis)

def _gelu(x):
    return jax.nn.gelu(x, approximate=True)

def _silu(x):
    return jax.nn.silu(x)

def _sigmoid(x):
    return jax.nn.sigmoid(x)

def _layernorm(x, axis=-1, eps=1e-05):
    m = jnp.mean(x, axis=axis, keepdims=True)
    v = jnp.var(x, axis=axis, keepdims=True)
    return (x - m) / jnp.sqrt(v + eps)

def _scatter_add(tgt, idx, src, axis=0):
    return tgt.at[idx].add(src)

def _segment_sum(src, seg, n):
    return jax.ops.segment_sum(src, seg, n)
kernel_name = 'mk_sandwich_d2_jaxref_r8_56850a'

def setup_inputs(seed: int=0):
    np.random.seed(seed)
    _w = jnp.asarray

    def _L0_attn_setup():
        import jax, jax.numpy as jnp
        import numpy as np
        H = 16

        def _eff_if_sorted(poids, Z):
            if poids.ndim == Z.ndim + 1:
                Zb = Z[..., None]
            else:
                Zb = Z
            a = jnp.cumsum(poids, axis=2)
            b = jnp.cumsum(poids * Zb, axis=2)
            return a * Zb - b
        key = jax.random.key(seed)
        ks = jax.random.split(key, 11)
        E = 128
        B, T = (4, 512)
        s = 1.0 / np.sqrt(E)
        return {'hidden_states': jax.random.normal(ks[0], (B, T, E), jnp.float32), 'Wq': jax.random.normal(ks[1], (E, E), jnp.float32) * s, 'bq': jax.random.normal(ks[2], (E,), jnp.float32) * 0.01, 'Wk': jax.random.normal(ks[3], (E, E), jnp.float32) * s, 'bk': jax.random.normal(ks[4], (E,), jnp.float32) * 0.01, 'Wv': jax.random.normal(ks[5], (E, E), jnp.float32) * s, 'bv': jax.random.normal(ks[6], (E,), jnp.float32) * 0.01, 'W1': jax.random.normal(ks[7], (E, E), jnp.float32) * s, 'b1': jax.random.normal(ks[8], (E,), jnp.float32) * 0.01, 'W2': jax.random.normal(ks[9], (E, H), jnp.float32) * s, 'b2': jax.random.normal(ks[10], (H,), jnp.float32) * 0.01}
    _L0_attn_in = _L0_attn_setup()

    def _L0_ffn_setup():
        import jax, jax.numpy as jnp
        import numpy as np
        TOPK = 4
        key = jax.random.key(seed)
        ks = jax.random.split(key, 9)
        B, T, D = (4, 256, 128)
        E, H = (32, 128)
        HS = H * TOPK
        s = lambda k, shape, fan: jax.random.normal(k, shape, dtype=jnp.float32) / np.sqrt(fan)
        return {'x': jax.random.normal(ks[0], (B, T, D), dtype=jnp.float32), 'router_w': s(ks[1], (E, D), D), 'router_bias': jnp.zeros((E,), dtype=jnp.float32), 'gate_w': s(ks[2], (E, H, D), D), 'up_w': s(ks[3], (E, H, D), D), 'down_w': s(ks[4], (E, D, H), H), 'sgate_w': s(ks[5], (HS, D), D), 'sup_w': s(ks[6], (HS, D), D), 'sdown_w': s(ks[7], (D, HS), HS)}
    _L0_ffn_in = _L0_ffn_setup()

    def _L1_attn_setup():
        import jax, jax.numpy as jnp
        import numpy as np
        B, T, C = (8, 256, 128)
        NL, LID = (12, 1)
        H = 4 * C

        def _ln(x, g, b):
            m = x.mean(-1, keepdims=True)
            v = ((x - m) ** 2).mean(-1, keepdims=True)
            return (x - m) * jax.lax.rsqrt(v + 1e-05) * g + b

        def _shift(x):
            return jnp.pad(x, ((0, 0), (1, 0), (0, 0)))[:, :-1]

        def _wkv(time_decay, time_first, k, v):
            w = -jnp.exp(time_decay)
            kt = jnp.moveaxis(k, 1, 0)
            vt = jnp.moveaxis(v, 1, 0)
            Bb, Cc = (k.shape[0], k.shape[2])
            init = (jnp.zeros((Bb, Cc), k.dtype), jnp.zeros((Bb, Cc), k.dtype), jnp.full((Bb, Cc), -1e+38, k.dtype))

            def step(carry, kv_t):
                aa, bb, pp = carry
                kk, vv = kv_t
                ww = time_first + kk
                p = jnp.maximum(pp, ww)
                e1 = jnp.exp(pp - p)
                e2 = jnp.exp(ww - p)
                out = (e1 * aa + e2 * vv) / (e1 * bb + e2)
                ww2 = pp + w
                p2 = jnp.maximum(ww2, kk)
                e1b = jnp.exp(ww2 - p2)
                e2b = jnp.exp(kk - p2)
                return ((e1b * aa + e2b * vv, e1b * bb + e2b, p2), out)
            _, out = jax.lax.scan(step, init, (kt, vt))
            return jnp.moveaxis(out, 0, 1)
        key = jax.random.key(seed)
        ks = jax.random.split(key, 8)
        f = lambda i, shape: 0.02 * jax.random.normal(ks[i], shape, jnp.float32)
        r01 = LID / (NL - 1)
        r10 = 1.0 - LID / NL
        h = np.arange(C, dtype=np.float64)
        decay = (-5 + 8 * (h / (C - 1)) ** (0.7 + 1.3 * r01)).astype(np.float32)
        zig = np.array([(i + 1) % 3 - 1 for i in range(C)]) * 0.5
        tfirst = (np.ones(C) * np.log(0.3) + zig).astype(np.float32)
        xpos = h / C
        tmk = (xpos ** r10).astype(np.float32)
        tmv = (xpos ** r10 + 0.3 * r01).astype(np.float32)
        tmr = (xpos ** (0.5 * r10)).astype(np.float32)
        cm = (xpos ** r10).astype(np.float32)
        return dict(x=jax.random.normal(ks[0], (B, T, C), jnp.float32), ln1_g=jnp.ones(C, jnp.float32), ln1_b=jnp.zeros(C, jnp.float32), ln2_g=jnp.ones(C, jnp.float32), ln2_b=jnp.zeros(C, jnp.float32), time_decay=jnp.asarray(decay), time_first=jnp.asarray(tfirst), time_mix_k=jnp.asarray(tmk), time_mix_v=jnp.asarray(tmv), time_mix_r=jnp.asarray(tmr), att_Wk=f(1, (C, C)), att_Wv=f(2, (C, C)), att_Wr=f(3, (C, C)), att_Wo=f(4, (C, C)), cm_k=jnp.asarray(cm), cm_r=jnp.asarray(cm), ffn_Wk=f(5, (H, C)), ffn_Wr=f(6, (C, C)), ffn_Wv=f(7, (C, H)))
    _L1_attn_in = _L1_attn_setup()

    def _L1_ffn_setup():
        import jax, jax.numpy as jnp
        import numpy as np
        D_MODEL = 128
        N_EXPERTS = 8
        TOP_K = 2
        HIDDEN = 4 * D_MODEL
        key = jax.random.key(seed)
        ks = jax.random.split(key, 6)
        B, S = (2, 256)
        x = jax.random.normal(ks[0], (B, S, D_MODEL), dtype=jnp.float32)
        shared_w1 = jax.random.normal(ks[1], (HIDDEN, D_MODEL), dtype=jnp.float32) * 0.02
        shared_w2 = jax.random.normal(ks[2], (D_MODEL, HIDDEN), dtype=jnp.float32) * 0.02
        experts_w1 = jax.random.normal(ks[3], (N_EXPERTS, HIDDEN, D_MODEL), dtype=jnp.float32) * 0.02
        experts_w2 = jax.random.normal(ks[4], (N_EXPERTS, D_MODEL, HIDDEN), dtype=jnp.float32) * 0.02
        gate_w = jax.random.normal(ks[5], (N_EXPERTS, D_MODEL), dtype=jnp.float32) * 0.02
        return {'x': x, 'shared_w1': shared_w1, 'shared_w2': shared_w2, 'experts_w1': experts_w1, 'experts_w2': experts_w2, 'gate_w': gate_w}
    _L1_ffn_in = _L1_ffn_setup()
    _d = {'L0_attn_hidden_states': _L0_attn_in['hidden_states'], 'L0_attn_Wq': _L0_attn_in['Wq'], 'L0_attn_bq': _L0_attn_in['bq'], 'L0_attn_Wk': _L0_attn_in['Wk'], 'L0_attn_bk': _L0_attn_in['bk'], 'L0_attn_Wv': _L0_attn_in['Wv'], 'L0_attn_bv': _L0_attn_in['bv'], 'L0_attn_W1': _L0_attn_in['W1'], 'L0_attn_b1': _L0_attn_in['b1'], 'L0_attn_W2': _L0_attn_in['W2'], 'L0_attn_b2': _L0_attn_in['b2'], 'L0_ffn_router_w': _L0_ffn_in['router_w'], 'L0_ffn_router_bias': _L0_ffn_in['router_bias'], 'L0_ffn_gate_w': _L0_ffn_in['gate_w'], 'L0_ffn_up_w': _L0_ffn_in['up_w'], 'L0_ffn_down_w': _L0_ffn_in['down_w'], 'L0_ffn_sgate_w': _L0_ffn_in['sgate_w'], 'L0_ffn_sup_w': _L0_ffn_in['sup_w'], 'L0_ffn_sdown_w': _L0_ffn_in['sdown_w'], 'L1_attn_ln1_g': _L1_attn_in['ln1_g'], 'L1_attn_ln1_b': _L1_attn_in['ln1_b'], 'L1_attn_ln2_g': _L1_attn_in['ln2_g'], 'L1_attn_ln2_b': _L1_attn_in['ln2_b'], 'L1_attn_time_decay': _L1_attn_in['time_decay'], 'L1_attn_time_first': _L1_attn_in['time_first'], 'L1_attn_time_mix_k': _L1_attn_in['time_mix_k'], 'L1_attn_time_mix_v': _L1_attn_in['time_mix_v'], 'L1_attn_time_mix_r': _L1_attn_in['time_mix_r'], 'L1_attn_att_Wk': _L1_attn_in['att_Wk'], 'L1_attn_att_Wv': _L1_attn_in['att_Wv'], 'L1_attn_att_Wr': _L1_attn_in['att_Wr'], 'L1_attn_att_Wo': _L1_attn_in['att_Wo'], 'L1_attn_cm_k': _L1_attn_in['cm_k'], 'L1_attn_cm_r': _L1_attn_in['cm_r'], 'L1_attn_ffn_Wk': _L1_attn_in['ffn_Wk'], 'L1_attn_ffn_Wr': _L1_attn_in['ffn_Wr'], 'L1_attn_ffn_Wv': _L1_attn_in['ffn_Wv'], 'L1_ffn_shared_w1': _L1_ffn_in['shared_w1'], 'L1_ffn_shared_w2': _L1_ffn_in['shared_w2'], 'L1_ffn_experts_w1': _L1_ffn_in['experts_w1'], 'L1_ffn_experts_w2': _L1_ffn_in['experts_w2'], 'L1_ffn_gate_w': _L1_ffn_in['gate_w']}
    _x0 = _d['L0_attn_hidden_states']
    _d['L0_attn_hidden_states'] = jax.random.normal(jax.random.fold_in(jax.random.key(seed), 1), (16, 256, 128), dtype=_x0.dtype)
    del _x0
    return _d

def reference(L0_attn_hidden_states, L0_attn_Wq, L0_attn_bq, L0_attn_Wk, L0_attn_bk, L0_attn_Wv, L0_attn_bv, L0_attn_W1, L0_attn_b1, L0_attn_W2, L0_attn_b2, L0_ffn_router_w, L0_ffn_router_bias, L0_ffn_gate_w, L0_ffn_up_w, L0_ffn_down_w, L0_ffn_sgate_w, L0_ffn_sup_w, L0_ffn_sdown_w, L1_attn_ln1_g, L1_attn_ln1_b, L1_attn_ln2_g, L1_attn_ln2_b, L1_attn_time_decay, L1_attn_time_first, L1_attn_time_mix_k, L1_attn_time_mix_v, L1_attn_time_mix_r, L1_attn_att_Wk, L1_attn_att_Wv, L1_attn_att_Wr, L1_attn_att_Wo, L1_attn_cm_k, L1_attn_cm_r, L1_attn_ffn_Wk, L1_attn_ffn_Wr, L1_attn_ffn_Wv, L1_ffn_shared_w1, L1_ffn_shared_w2, L1_ffn_experts_w1, L1_ffn_experts_w2, L1_ffn_gate_w):

    def _L0_attn_ref(hidden_states, Wq, bq, Wk, bk, Wv, bv, W1, b1, W2, b2):
        import jax, jax.numpy as jnp
        import numpy as np
        H = 16

        def _eff_if_sorted(poids, Z):
            if poids.ndim == Z.ndim + 1:
                Zb = Z[..., None]
            else:
                Zb = Z
            a = jnp.cumsum(poids, axis=2)
            b = jnp.cumsum(poids * Zb, axis=2)
            return a * Zb - b
        B, T, E = hidden_states.shape
        D = E // H

        def heads(x):
            return x.reshape(B, T, H, D).transpose(0, 2, 1, 3)
        q = heads(hidden_states @ Wq + bq)
        k = heads(hidden_states @ Wk + bk)
        v = heads(hidden_states @ Wv + bv)

        def proj(x4):
            x = x4.reshape(B, T, H * D)
            m = jax.nn.gelu(x @ W1 + b1, approximate=False)
            return m @ W2 + b2
        q_proj = proj(q)
        k_proj = proj(k)
        eps = 1e-06
        mean_q = jnp.mean(q_proj, axis=1, keepdims=True)
        mean_k = jnp.mean(k_proj, axis=1, keepdims=True)
        qc = q_proj - mean_q
        kc = k_proj - mean_k
        var_q = jnp.mean(qc ** 2, axis=1, keepdims=True)
        var_k = jnp.mean(kc ** 2, axis=1, keepdims=True)
        std = jnp.sqrt(0.5 * (var_q + var_k) + eps)
        q_proj = qc / std
        k_proj = kc / std
        Z = jnp.concatenate([k_proj, q_proj], axis=1).transpose(0, 2, 1)
        idx = jnp.argsort(Z, axis=2)
        Z_sort = jnp.take_along_axis(Z, idx, axis=2)
        inv = jnp.argsort(idx, axis=2)
        vc = v - jnp.mean(v, axis=2, keepdims=True)
        v_exp = jnp.concatenate([vc, jnp.zeros_like(vc)], axis=2)
        v_sorted = jnp.take_along_axis(v_exp, idx[..., None], axis=2)
        context_s = _eff_if_sorted(v_sorted, Z_sort)
        context = jnp.take_along_axis(context_s, inv[..., None], axis=2)[:, :, T:]
        v_norm = jnp.concatenate([jnp.ones((B, H, T), Z.dtype), jnp.zeros((B, H, T), Z.dtype)], axis=2)
        vns = jnp.take_along_axis(v_norm, idx, axis=2)
        sum_relu = _eff_if_sorted(vns, Z_sort)
        total_v = jnp.sum(vns, axis=2, keepdims=True)
        total_vz = jnp.sum(vns * Z_sort, axis=2, keepdims=True)
        norm_sorted = 2.0 * sum_relu - (Z_sort * total_v - total_vz)
        norm = jnp.take_along_axis(norm_sorted, inv, axis=2)[:, :, T:]
        norm = jnp.maximum(norm, 0.0001)
        context = 2.0 * context / norm[..., None]
        return context.transpose(0, 2, 1, 3).reshape(B, T, H * D)

    def _L0_ffn_ref(x, router_w, router_bias, gate_w, up_w, down_w, sgate_w, sup_w, sdown_w):
        import jax, jax.numpy as jnp
        import numpy as np
        TOPK = 4
        B, T, D = x.shape
        flat = x.reshape(B * T, D)
        logits = flat.astype(jnp.float32) @ router_w.T + router_bias
        scores = jax.nn.softmax(logits, axis=-1)
        topk_scores, topk_idx = jax.lax.top_k(scores, TOPK)
        topk_scores = topk_scores / jnp.clip(topk_scores.sum(axis=-1, keepdims=True), 1e-12, None)
        h = jax.nn.silu(jnp.einsum('nd,ehd->neh', flat, gate_w)) * jnp.einsum('nd,ehd->neh', flat, up_w)
        expert_out = jnp.einsum('neh,edh->ned', h, down_w)
        sel = jnp.take_along_axis(expert_out, topk_idx[:, :, None], axis=1)
        out = (sel * topk_scores.astype(flat.dtype)[:, :, None]).sum(axis=1)
        out = out + jax.nn.silu(flat @ sgate_w.T) * (flat @ sup_w.T) @ sdown_w.T
        return out.reshape(B, T, D)

    def _L1_attn_ref(x, ln1_g, ln1_b, ln2_g, ln2_b, time_decay, time_first, time_mix_k, time_mix_v, time_mix_r, att_Wk, att_Wv, att_Wr, att_Wo, cm_k, cm_r, ffn_Wk, ffn_Wr, ffn_Wv):
        import jax, jax.numpy as jnp
        import numpy as np
        B, T, C = (8, 256, 128)
        NL, LID = (12, 1)
        H = 4 * C

        def _ln(x, g, b):
            m = x.mean(-1, keepdims=True)
            v = ((x - m) ** 2).mean(-1, keepdims=True)
            return (x - m) * jax.lax.rsqrt(v + 1e-05) * g + b

        def _shift(x):
            return jnp.pad(x, ((0, 0), (1, 0), (0, 0)))[:, :-1]

        def _wkv(time_decay, time_first, k, v):
            w = -jnp.exp(time_decay)
            kt = jnp.moveaxis(k, 1, 0)
            vt = jnp.moveaxis(v, 1, 0)
            Bb, Cc = (k.shape[0], k.shape[2])
            init = (jnp.zeros((Bb, Cc), k.dtype), jnp.zeros((Bb, Cc), k.dtype), jnp.full((Bb, Cc), -1e+38, k.dtype))

            def step(carry, kv_t):
                aa, bb, pp = carry
                kk, vv = kv_t
                ww = time_first + kk
                p = jnp.maximum(pp, ww)
                e1 = jnp.exp(pp - p)
                e2 = jnp.exp(ww - p)
                out = (e1 * aa + e2 * vv) / (e1 * bb + e2)
                ww2 = pp + w
                p2 = jnp.maximum(ww2, kk)
                e1b = jnp.exp(ww2 - p2)
                e2b = jnp.exp(kk - p2)
                return ((e1b * aa + e2b * vv, e1b * bb + e2b, p2), out)
            _, out = jax.lax.scan(step, init, (kt, vt))
            return jnp.moveaxis(out, 0, 1)
        xa = _ln(x, ln1_g, ln1_b)
        xx = _shift(xa)
        xk = xa * time_mix_k + xx * (1 - time_mix_k)
        xv = xa * time_mix_v + xx * (1 - time_mix_v)
        xr = xa * time_mix_r + xx * (1 - time_mix_r)
        k = jnp.einsum('btc,oc->bto', xk, att_Wk)
        v = jnp.einsum('btc,oc->bto', xv, att_Wv)
        r = jnp.einsum('btc,oc->bto', xr, att_Wr)
        rwkv = jax.nn.sigmoid(r) * _wkv(time_decay, time_first, k, v)
        x = x + jnp.einsum('bto,co->btc', rwkv, att_Wo)
        xc = _ln(x, ln2_g, ln2_b)
        xx2 = _shift(xc)
        xk2 = xc * cm_k + xx2 * (1 - cm_k)
        xr2 = xc * cm_r + xx2 * (1 - cm_r)
        kk = jnp.square(jax.nn.relu(jnp.einsum('btc,hc->bth', xk2, ffn_Wk)))
        kv = jnp.einsum('bth,ch->btc', kk, ffn_Wv)
        rkv = jax.nn.sigmoid(jnp.einsum('btc,oc->bto', xr2, ffn_Wr)) * kv
        return x + rkv

    def _L1_ffn_ref(x, shared_w1, shared_w2, experts_w1, experts_w2, gate_w):
        import jax, jax.numpy as jnp
        import numpy as np
        D_MODEL = 128
        N_EXPERTS = 8
        TOP_K = 2
        HIDDEN = 4 * D_MODEL
        B, S, D = x.shape
        T = B * S
        x_flat = x.reshape(T, D)
        shared = jnp.einsum('td,dh->th', x_flat, shared_w1.T)
        shared = jnp.einsum('th,hd->td', jax.nn.silu(shared), shared_w2.T)
        gate_logits = x_flat @ gate_w.T
        top_k_gates, top_k_idx = jax.lax.top_k(gate_logits, TOP_K)
        top_k_gates = jax.nn.softmax(top_k_gates, axis=1)
        gates = jnp.zeros((T, N_EXPERTS), dtype=x.dtype)
        gates = gates.at[jnp.arange(T)[:, None], top_k_idx].set(top_k_gates)
        h = jnp.einsum('td,ehd->teh', x_flat, experts_w1)
        expert_out = jnp.einsum('teh,edh->ted', jax.nn.silu(h), experts_w2)
        selected = jnp.einsum('ted,te->td', expert_out, gates)
        return (shared + selected).reshape(B, S, D)
    x = L0_attn_hidden_states
    x = x + _layernorm(_L0_attn_ref(_layernorm(x, axis=-1), L0_attn_Wq, L0_attn_bq, L0_attn_Wk, L0_attn_bk, L0_attn_Wv, L0_attn_bv, L0_attn_W1, L0_attn_b1, L0_attn_W2, L0_attn_b2), axis=-1)
    x = x + _layernorm(_L0_ffn_ref(_layernorm(x, axis=-1), L0_ffn_router_w, L0_ffn_router_bias, L0_ffn_gate_w, L0_ffn_up_w, L0_ffn_down_w, L0_ffn_sgate_w, L0_ffn_sup_w, L0_ffn_sdown_w), axis=-1)
    x = x + _layernorm(_L1_attn_ref(_layernorm(x, axis=-1), L1_attn_ln1_g, L1_attn_ln1_b, L1_attn_ln2_g, L1_attn_ln2_b, L1_attn_time_decay, L1_attn_time_first, L1_attn_time_mix_k, L1_attn_time_mix_v, L1_attn_time_mix_r, L1_attn_att_Wk, L1_attn_att_Wv, L1_attn_att_Wr, L1_attn_att_Wo, L1_attn_cm_k, L1_attn_cm_r, L1_attn_ffn_Wk, L1_attn_ffn_Wr, L1_attn_ffn_Wv), axis=-1)
    x = x + _layernorm(_L1_ffn_ref(_layernorm(x, axis=-1), L1_ffn_shared_w1, L1_ffn_shared_w2, L1_ffn_experts_w1, L1_ffn_experts_w2, L1_ffn_gate_w), axis=-1)
    return x

_drawn_inputs = setup_inputs


def setup_inputs(seed=0):
    import zlib

    import numpy as np

    out = dict(_drawn_inputs(seed))
    spreads = {'L0_ffn_router_bias': (0.0, 0.1),
     'L1_attn_ln1_g': (1.0, 0.6),
     'L1_attn_ln1_b': (0.0, 0.8),
     'L1_attn_ln2_g': (1.0, 0.6),
     'L1_attn_ln2_b': (0.0, 0.8)}
    factors = {'L0_attn_bv': 8.0,
     'L0_attn_b2': 8.0,
     'L1_attn_time_decay': 6.086,
     'L1_attn_time_first': 8.0,
     'L1_attn_time_mix_k': 8.0,
     'L1_attn_time_mix_v': 7.446,
     'L1_attn_time_mix_r': 8.0,
     'L1_attn_att_Wk': 8.0,
     'L1_attn_att_Wv': 3.422,
     'L1_attn_att_Wr': 8.0,
     'L1_attn_att_Wo': 3.264,
     'L1_attn_cm_k': 7.016,
     'L1_attn_cm_r': 8.0,
     'L1_attn_ffn_Wk': 4.538,
     'L1_attn_ffn_Wr': 8.0,
     'L1_attn_ffn_Wv': 4.788}
    for name, (base, spread) in spreads.items():
        noise = np.random.default_rng([zlib.crc32(name.encode()), seed]).standard_normal(out[name].shape)
        drawn = base * np.exp(spread * noise) if base else spread * noise
        out[name] = jnp.asarray(drawn.astype(out[name].dtype))
    for name, factor in factors.items():
        out[name] = (out[name] * factor).astype(out[name].dtype)
    return out
```

```python
import itertools
from contextlib import ExitStack

import numpy as np
import concourse.bass as bass
from concourse import mybir

F32 = mybir.dt.float32
F32R = mybir.dt.float32r
BF16 = mybir.dt.bfloat16
ALU = mybir.AluOpType
ACT = mybir.ActivationFunctionType
AX = mybir.AxisListType

P = 128
NB, T = 16, 256
TILES = NB * T // P
GROUPS = 8
TPG = TILES // GROUPS
GW = TPG * P
BPG = GW // T
TPB = T // P
N = TILES * P

HEADS, HD = 16, 8
HR = 32
LO, HI = 16, 16
VC = 2 * HD + 2
PARTS = 3
HQ = 4

E0, K0, SH0 = 32, 4, 4
E1, K1, CH1 = 8, 2, 4
CH_RWKV = 4
LN_EPS = 1e-5
STD_EPS = 1e-6
FROM = 1
NEVER = -1e38
OUTSIDE = -3e38


def at(tile, start, size=P):
    return tile[:, bass.ds(start, size)]


class Chain:

    def __init__(self, eng, sem, base=0):
        self.eng, self.sem, self.base, self.n = eng, sem, base, 0

    def mark(self, ins):
        self.n += 1
        ins.then_inc(self.sem, 1)

    def wait(self):
        self.eng.wait_ge(self.sem, FROM + self.base + self.n)

    def link(self, ins):
        self.mark(ins)
        self.wait()


def build(nc, a, out):
    top = ExitStack()
    with top:
        def keep(name, cols, dt=F32, rows=P):
            return top.enter_context(nc.sbuf_tensor(name, [rows, cols], dt))

        ready = []
        taken = []

        def ready_semaphores(n):
            engines = (nc.sync, nc.scalar, nc.vector, nc.gpsimd, nc.tensor)
            for i in range(n):
                ready.append(nc.alloc_semaphore(f"ready_{next(serial)}"))
                engines[i % len(engines)].sem_inc(ready[-1], FROM)
            nc.all_engine_barrier()

        def semaphore(name):
            taken.append(ready.pop())
            return taken[-1]

        def clear_semaphores(n):
            nc.clear_and_free_semaphores(taken + ready)
            taken.clear()
            ready.clear()
            nc.all_engine_barrier()
            ready_semaphores(n)

        serial = itertools.count()
        ready_semaphores(100)
        x_tok = keep("x_tok", N)
        y_tok = keep("y_tok", N)
        h_tok = keep("h_tok", N)
        ident = keep("ident", P)
        ones = keep("ones", P)
        eps_ln = keep("eps_ln", 1)
        eps_std = keep("eps_std", 1)
        stats = keep("stats", TILES * 6)
        mean = keep("mean", TILES)
        rstd = keep("rstd", TILES)
        spread = keep("spread", TILES)

        def row_stats(dve, src, done):
            with dve.Fori(0, GROUPS) as g:
                for t in range(TPG):
                    nc.vector.bn_stats(at(stats, g * (TPG * 6) + t * 6, 6),
                                       at(src, g * GW + t * P)).then_inc(done, 1)
            dve.wait_ge(done, FROM + TILES)

        def merge_stats(c, st, mean_, var_, tmp_, count):
            s = st.rearrange("p (t s) -> p t s", s=6)
            c.mark(nc.vector.tensor_tensor(mean_, s[:, :, 1], s[:, :, 4], ALU.add))
            c.link(nc.vector.tensor_tensor(tmp_, s[:, :, 1], s[:, :, 4], ALU.subtract))
            c.mark(nc.vector.tensor_scalar(mean_, mean_, 0.5, None, ALU.mult))
            c.link(nc.vector.tensor_tensor(tmp_, tmp_, tmp_, ALU.mult))
            c.mark(nc.vector.tensor_tensor(var_, s[:, :, 2], s[:, :, 5], ALU.add))
            c.link(nc.vector.tensor_scalar(tmp_, tmp_, count / 2, None, ALU.mult))
            c.link(nc.vector.tensor_tensor(var_, var_, tmp_, ALU.add))

        def norm_dve(dve, c, src, stats_done, var_ready, std_ready):
            row_stats(dve, src, stats_done)
            merge_stats(c, stats[:, :], mean[:, :], rstd[:, :], spread[:, :], P // 2)
            dve.sem_inc(var_ready, 1)
            dve.wait_ge(std_ready, FROM + 1)
            c.link(nc.vector.reciprocal(rstd[:, :], rstd[:, :]))

        def norm_act(act, var_ready, std_ready):
            act.wait_ge(var_ready, FROM + 1)
            nc.scalar.activation(rstd[:, :], rstd[:, :], ACT.Sqrt, bias=eps_ln[:, :],
                                 scale=1.0 / P).then_inc(std_ready, 1)

        def norm_rows(dve, src, dst, done, tiles=TPG):
            with dve.Fori(0, GROUPS) as g:
                for t in range(TPG):
                    last = nc.vector.tensor_scalar(
                        at(dst, g * GW + t * P), at(src, g * GW + t * P),
                        at(mean, g * TPG + t, 1), at(rstd, g * TPG + t, 1), ALU.subtract, ALU.mult)
                last.then_inc(done, 1)

        def transposes(pe, src, banks, ready, done, evacuated):
            for g in range(GROUPS):
                pe.wait_ge(ready, FROM + g + 1)
                if g >= 2:
                    pe.wait_ge(evacuated, FROM + g - 1)
                for t in range(TPG):
                    o = (g * TPG + t) * P
                    last = nc.tensor.transpose(banks[g % 2][:, t * P:(t + 1) * P], src[:, o:o + P], ident[:, :])
                last.then_inc(done, 1)

        with ExitStack() as s:
            loaded, made = semaphore("x_loaded"), semaphore("constants_made")
            with nc.Block() as block:
                @block.sync
                def _(sp):
                    sp.dma_start(x_tok[:, :].rearrange("p (b u c) -> p b u c", u=TPB, c=P),
                                 a["x"].rearrange("b (u p) c -> p b u c", p=P)).then_inc(loaded, 16)
                    sp.wait_ge(loaded, FROM + 16)

                @block.vector
                def _(dve):
                    nc.vector.memset(ones[:, :], 1.0)
                    nc.vector.memset(eps_ln[:, :], LN_EPS)
                    nc.vector.memset(eps_std[:, :], STD_EPS)

                @block.gpsimd
                def _(pool):
                    nc.gpsimd.memset(ident[:, :], 0.0).then_inc(made, 1)
                    pool.wait_ge(made, FROM + 1)
                    nc.gpsimd.affine_select(out=ident[:, :], in_=ident[:, :], compare_op=ALU.not_equal,
                                            fill=1.0, base=0, pattern=[[-1, P]], channel_multiplier=1)

        attention0(nc, a, locals())
        add_normed(nc, locals())
        experts(nc, a, locals(), 0)
        add_normed(nc, locals())
        clear_semaphores(90)
        rwkv(nc, a, locals())
        add_normed(nc, locals())
        clear_semaphores(50)
        experts(nc, a, locals(), 1)
        add_normed(nc, locals())

        with nc.semaphore("stored") as stored, nc.Block() as block:
            @block.sync
            def _(sp):
                sp.dma_start(out.rearrange("b (u p) c -> p b u c", p=P),
                             x_tok[:, :].rearrange("p (b u c) -> p b u c", u=TPB, c=P)).then_inc(stored, 16)
                sp.wait_ge(stored, 16)


def add_normed(nc, env):
    x_tok, y_tok = env["x_tok"], env["y_tok"]
    with ExitStack() as s:
        sem = lambda n: env["semaphore"](n)
        stats_done, self_done, var_ready, std_ready, normed = map(
            sem, ("stats_done", "dve_done", "var_ready", "std_ready", "normed"))
        with nc.Block() as block:
            @block.vector
            def _(dve):
                c = Chain(dve, self_done)
                env["norm_dve"](dve, c, y_tok, stats_done, var_ready, std_ready)
                env["norm_rows"](dve, y_tok, y_tok, normed)

            @block.scalar
            def _(act):
                env["norm_act"](act, var_ready, std_ready)

            @block.gpsimd
            def _(pool):
                with pool.Fori(0, GROUPS) as g:
                    pool.wait_ge(normed, FROM + g + 1)
                    nc.gpsimd.tensor_tensor(at(x_tok, g * GW, GW), at(x_tok, g * GW, GW),
                                            at(y_tok, g * GW, GW), ALU.add)


def attention0(nc, a, env):
    x_tok, y_tok, h_tok = env["x_tok"], env["y_tok"], env["h_tok"]
    ident, ones, eps_std = env["ident"], env["ones"], env["eps_std"]
    phase = ExitStack()
    with phase:
        def sb(name, cols, dt=F32, rows=P):
            return phase.enter_context(nc.sbuf_tensor(name, [rows, cols], dt))

        PR = 2 * HR
        proj = {"q": sb("proj_q", N, rows=PR), "k": sb("proj_k", N, rows=PR)}
        pstat = {w: sb(f"pstat_{w}", NB * 6, rows=PR) for w in "qk"}
        pmean = {w: sb(f"pmean_{w}", NB, rows=PR) for w in "qk"}
        pvar = {w: sb(f"pvar_{w}", NB, rows=PR) for w in "qk"}
        ptmp = sb("ptmp", NB, rows=PR)
        v_tok = sb("v_tok", N)

        with ExitStack() as s:
            def tb(name, cols, dt=F32, rows=P):
                return s.enter_context(nc.sbuf_tensor(name, [rows, cols], dt))
            sem = lambda n: env["semaphore"](n)
            ps = [s.enter_context(nc.psum_tensor(f"ps{i}", [P, GW], F32)) for i in range(8)]
            w = {n: tb(f"w_{n}", P) for n in ("Wv", "W1")}
            w_qk = tb("w_qk", 2 * P)
            b_qk = tb("b_qk", 2 * P)
            w2 = tb("w2", PR)
            b = {n: tb(f"b_{n}", 1) for n in ("bv", "b1")}
            b2 = tb("b2", 1, rows=PR)
            h_fm = tb("h_fm", N)
            qk_tok = tb("qk_tok", LO * 2 * P)
            rows_fm = {"q": h_tok, "k": y_tok}
            v_fm, v_cent = tb("v_fm", GW), tb("v_cent", GW)
            gelu = {x: tb(f"gelu_{x}", GW) for x in "qk"}
            vstat, vmean = tb("vstat", BPG * 6), tb("vmean", BPG)
            weights, cleared = sem("weights"), sem("w2_cleared")
            WLOADS = len(w) + len(b) + 4 + 4
            stats_done, self_done, var_ready, std_ready = map(
                sem, ("stats_done", "dve_done", "var_ready", "std_ready"))
            rows_ready, fm_ps, fm_sb = sem("rows_ready"), sem("fm_ps"), sem("fm_sb")
            v_ps, v_sb = sem("v_ps"), sem("v_sb")
            qk_ps, qk_sb, turned_ps, turned_sb = map(sem, ("qk_ps", "qk_sb", "turned_ps", "turned_sb"))
            up_ps = {x: sem(f"up_{x}_ps") for x in "qk"}
            up_sb = {x: sem(f"up_{x}_sb") for x in "qk"}
            pr_ps = {x: sem(f"pr_{x}_ps") for x in "qk"}
            pr_sb = {x: sem(f"pr_{x}_sb") for x in "qk"}
            v_self, centred, vt_ps, vt_sb = sem("v_self"), sem("centred"), sem("vt_ps"), sem("vt_sb")
            NQ = LO // 2
            NTURN = 2 * HEADS // TPG
            up = {"q": ps[3], "k": ps[4]}
            down = {"q": ps[5], "k": ps[6]}
            with nc.Block() as block:
                @block.sync
                def _(sp):
                    for n in w:
                        sp.dma_start(w[n][:, :], a[n]).then_inc(weights, 16)
                    for n in b:
                        sp.dma_start(b[n][:, :], a[n]).then_inc(weights, 16)
                    for i, n in enumerate("qk"):
                        sp.dma_start(w_qk[:, i * P:(i + 1) * P], a["W" + n]).then_inc(weights, 16)
                        sp.dma_start(b_qk[:, i * P:(i + 1) * P],
                                     a["b" + n].rearrange("c o -> o c").partition_broadcast(P)).then_inc(weights, 16)
                    sp.wait_ge(cleared, FROM + 2)
                    for r in range(2):
                        sp.dma_start(w2[:, r * HR:r * HR + HEADS], a["W2"]).then_inc(weights, 16)
                        sp.dma_start(b2[r * HR:r * HR + HEADS, :], a["b2"]).then_inc(weights, 16)

                @block.gpsimd
                def _(pool):
                    nc.gpsimd.memset(w2[:, :], 0.0).then_inc(cleared, 1)
                    nc.gpsimd.memset(b2[:, :], 0.0).then_inc(cleared, 1)

                @block.tensor
                def _(pe):
                    env["transposes"](pe, h_tok, ps[6:8], rows_ready, fm_ps, fm_sb)
                    pe.wait_ge(weights, FROM + WLOADS * 16)
                    pe.wait_ge(fm_sb, FROM + GROUPS)
                    hf = h_fm[:, :].rearrange("p (b t l) -> p l b t", t=HI, l=LO)
                    for half in range(2):
                        if half:
                            pe.wait_ge(turned_ps, FROM + NTURN)
                        for i in range(NQ):
                            n = half * NQ + i
                            if n >= 2:
                                pe.wait_ge(qk_sb, FROM + n - 1)
                            for l in range(2):
                                last = nc.tensor.matmul(ps[n % 2][:, l * 2 * P:(l + 1) * 2 * P],
                                                        hf[:, 2 * i + l, half * NB // 2:(half + 1) * NB // 2, :],
                                                        w_qk[:, :], start=True, stop=True)
                            last.then_inc(qk_ps, 1)
                        pe.wait_ge(qk_sb, FROM + (half + 1) * NQ)
                        for i in range(NTURN):
                            n = half * NTURN + i
                            if n >= 2:
                                pe.wait_ge(turned_sb, FROM + n - 1)
                            for t in range(TPG):
                                o = (i * TPG + t) * P
                                last = nc.tensor.transpose(ps[2 + n % 2][:, t * P:(t + 1) * P],
                                                           qk_tok[:, o:o + P], ident[:, :])
                            last.then_inc(turned_ps, 1)
                    pe.wait_ge(turned_sb, FROM + 2 * NTURN)
                    with pe.Fori(0, GROUPS) as g:
                        pe.wait_ge(v_sb, FROM + g)
                        nc.tensor.matmul(ps[2][:, :], w["Wv"][:, :], at(h_fm, g * GW, GW),
                                         start=True, stop=True).then_inc(v_ps, 1)
                        for x in "qk":
                            pe.wait_ge(up_sb[x], FROM + g)
                            nc.tensor.matmul(up[x][:, :], w["W1"][:, :], at(rows_fm[x], g * GW, GW),
                                             start=True, stop=True).then_inc(up_ps[x], 1)
                        pe.wait_ge(centred, FROM + g + 1)
                        pe.wait_ge(vt_sb, FROM + g)
                        for t in range(TPG):
                            last = nc.tensor.transpose(ps[7][:, t * P:(t + 1) * P],
                                                       v_cent[:, t * P:(t + 1) * P], ident[:, :])
                        last.then_inc(vt_ps, 1)
                        for x in "qk":
                            pe.wait_ge(up_sb[x], FROM + g + 1)
                            pe.wait_ge(pr_sb[x], FROM + g)
                            nc.tensor.matmul(down[x][0:PR, :], w2[:, :], gelu[x][:, :],
                                             start=True, stop=True).then_inc(pr_ps[x], 1)

                @block.scalar
                def _(act):
                    env["norm_act"](act, var_ready, std_ready)
                    with act.Fori(0, GROUPS // 2) as g2:
                        for u in range(2):
                            act.wait_ge(fm_ps, FROM + g2 * 2 + u + 1)
                            nc.scalar.activation(at(h_fm, g2 * (2 * GW) + u * GW, GW), ps[6 + u][:, :],
                                                 ACT.Copy).then_inc(fm_sb, 1)
                    for n in range(2 * NTURN):
                        half, x, hq = n // NTURN, n % NTURN // (NTURN // 2), n % (NTURN // 2)
                        act.wait_ge(turned_ps, FROM + n + 1)
                        dst = rows_fm["qk"[x]][:, :].rearrange("p (b h t) -> p h b t", h=HEADS, t=HI)
                        nc.scalar.activation(
                            dst[:, hq * TPG:(hq + 1) * TPG, half * NB // 2:(half + 1) * NB // 2, :],
                            ps[2 + n % 2][:, :].rearrange("p (h b t) -> p h b t", h=TPG, t=HI),
                            ACT.Copy).then_inc(turned_sb, 1)
                    act.wait_ge(weights, FROM + WLOADS * 16)
                    with act.Fori(0, GROUPS) as g:
                        for x in "qk":
                            act.wait_ge(up_ps[x], FROM + g + 1)
                            act.wait_ge(pr_ps[x], FROM + g)
                            nc.scalar.activation(gelu[x][:, :], up[x][:, :], ACT.Gelu,
                                                 bias=b["b1"][:, :]).then_inc(up_sb[x], 1)

                @block.vector
                def _(dve):
                    c = Chain(dve, self_done)
                    env["norm_dve"](dve, c, x_tok, stats_done, var_ready, std_ready)
                    env["norm_rows"](dve, x_tok, h_tok, rows_ready)
                    dve.wait_ge(weights, FROM + WLOADS * 16)
                    for n in range(2 * NQ):
                        half, i = n // NQ, n % NQ
                        dve.wait_ge(qk_ps, FROM + n + 1)
                        if half:
                            dve.wait_ge(turned_ps, FROM + NTURN)
                        nc.vector.tensor_tensor(
                            qk_tok[:, :].rearrange("p (h l d) -> p l h d", l=LO, d=HD)[:, 2 * i:2 * i + 2],
                            ps[n % 2][:, :].rearrange("p (l h d) -> p l h d", l=2, d=HD),
                            b_qk[:, :].rearrange("p (h d) -> p h d", d=HD).unsqueeze(1).broadcast_to(
                                [P, 2, 2 * HEADS, HD]), ALU.add).then_inc(qk_sb, 1)
                    steps = 6 + 2 * BPG
                    with dve.Fori(0, GROUPS) as g:
                        c = Chain(dve, v_self, g * steps)
                        dve.wait_ge(v_ps, FROM + g + 1)
                        nc.vector.tensor_scalar(v_fm[:, :], ps[2][:, :], b["bv"][:, :], None,
                                                ALU.add).then_inc(v_sb, 1)
                        dve.wait_ge(v_sb, FROM + g + 1)
                        for i in range(BPG):
                            c.mark(nc.vector.bn_stats(vstat[:, i * 6:i * 6 + 6], v_fm[:, i * T:(i + 1) * T]))
                        c.wait()
                        sv = vstat[:, :].rearrange("p (t s) -> p t s", s=6)
                        c.link(nc.vector.tensor_tensor(vmean[:, :], sv[:, :, 1], sv[:, :, 4], ALU.add))
                        c.link(nc.vector.tensor_scalar(vmean[:, :], vmean[:, :], 0.5, None, ALU.mult))
                        dve.wait_ge(vt_ps, FROM + g)
                        for i in range(BPG):
                            last = nc.vector.tensor_scalar(v_cent[:, i * T:(i + 1) * T], v_fm[:, i * T:(i + 1) * T],
                                                           vmean[:, i:i + 1], None, ALU.subtract)
                            c.mark(last)
                        c.wait()
                        dve.sem_inc(centred, 1)
                        dve.wait_ge(vt_ps, FROM + g + 1)
                        nc.vector.tensor_copy(at(v_tok, g * GW, GW), ps[7][:, :]).then_inc(vt_sb, 1)
                        for x in "qk":
                            dve.wait_ge(pr_ps[x], FROM + g + 1)
                            nc.vector.tensor_scalar(at(proj[x], g * GW, GW), down[x][0:PR, :], b2[:, :], None,
                                                    ALU.add).then_inc(pr_sb[x], 1)
                        for x in "qk":
                            dve.wait_ge(pr_sb[x], FROM + g + 1)
                            for i in range(BPG):
                                ins = nc.vector.bn_stats(at(pstat[x], g * (BPG * 6) + i * 6, 6),
                                                         at(proj[x], g * GW + i * T, T))
                                c.mark(ins)
                        assert c.n <= steps
                        while c.n < steps:
                            dve.sem_inc(v_self, 1)
                            c.n += 1
                        c.wait()

        with ExitStack() as s:
            def tb(name, cols, dt=F32, rows=P):
                return s.enter_context(nc.sbuf_tensor(name, [rows, cols], dt))
            sem = lambda n: env["semaphore"](n)
            psq = [s.enter_context(nc.psum_tensor(f"ps_q{i}", [P, HQ * T], F32)) for i in range(2)]
            pso = [s.enter_context(nc.psum_tensor(f"ps_o{i}", [P, GW], F32)) for i in range(2 * TPB)]
            q_parts = tb("q_parts", N, F32R)
            pick = tb("pick", HEADS * P, F32R)
            q_tok, k_tok = tb("q_tok", TILES * HEADS), tb("k_tok", TILES * HEADS)
            k_sum = tb("k_sum", NB * HEADS)
            qn, kn = tb("qn", T), tb("kn", T)
            hi_r = tb("hi_r", T, F32R, rows=PR)
            cols = tb("cols", HEADS * VC)
            rest = tb("rest", HEADS * VC)
            vals = [tb(f"vals{i}", TPB * HEADS * PARTS * VC, BF16) for i in range(2)]
            mask = [[tb(f"mask{i}{j}", HQ * T, BF16) for j in range(TPB)] for i in range(2)]
            sums = tb("sums", TPB * HEADS * VC)
            num = tb("num", T)
            n1, n2 = tb("n1", TPB * HEADS), tb("n2", TPB * HEADS)
            self_done, var_ready, std_ready = map(sem, ("dve_done", "var_ready", "std_ready"))
            prep, qk_rows, qk_ps, qk_sb = sem("prep"), sem("qk_rows"), sem("qk_ps"), sem("qk_sb")
            ksum_ps, ksum_sb = sem("ksum_ps"), sem("ksum_sb")
            pick_made, rows_cleared = sem("pick_made"), sem("rows_cleared")
            cols_self, cols_ready, hi_ready, mid_ready, rest_ready = map(
                sem, ("cols_self", "cols_ready", "hi_ready", "mid_ready", "rest_ready"))
            vals_ready = sem("vals_ready")
            q_ps, mask_ready, masked, sums_out, vals_used = map(
                sem, ("q_ps", "mask_ready", "masked", "sums_out", "vals_used"))
            batch_self = sem("batch_self")
            HALF = HEADS // 2
            HV = PARTS * VC
            with nc.Block() as block:
                @block.vector
                def _(dve):
                    c = Chain(dve, self_done)
                    for x in "qk":
                        env["merge_stats"](c, pstat[x][:, :], pmean[x][:, :], pvar[x][:, :], ptmp[:, :], T // 2)
                    c.link(nc.vector.tensor_tensor(pvar["q"][:, :], pvar["q"][:, :], pvar["k"][:, :], ALU.add))
                    dve.sem_inc(var_ready, 1)
                    dve.wait_ge(std_ready, FROM + 1)
                    c.link(nc.vector.reciprocal(pvar["q"][:, :], pvar["q"][:, :]))
                    rs = pvar["q"]
                    steps = 4
                    with dve.Fori(0, NB) as b_:
                        c = Chain(dve, prep, b_ * steps)
                        dve.wait_ge(qk_ps, FROM + b_)
                        c.mark(nc.vector.tensor_scalar(qn[0:PR, :], at(proj["q"], b_ * T, T), at(pmean["q"], b_, 1),
                                                       at(rs, b_, 1), ALU.subtract, ALU.mult))
                        c.link(nc.vector.tensor_scalar(kn[0:PR, :], at(proj["k"], b_ * T, T), at(pmean["k"], b_, 1),
                                                       at(rs, b_, 1), ALU.subtract, ALU.mult))
                        dve.sem_inc(qk_rows, 1)
                        nc.vector.tensor_copy(q_parts[0:HR, bass.ds(b_ * T, T)], qn[0:HR, :])
                        c.link(nc.vector.tensor_copy(hi_r[HR:PR, :], qn[HR:PR, :]))
                        c.link(nc.vector.tensor_tensor(q_parts[HR:PR, bass.ds(b_ * T, T)], qn[HR:PR, :],
                                                       hi_r[HR:PR, :].bitcast(F32), ALU.subtract))
                        assert c.n == steps
                    steps = 11
                    with dve.Fori(0, NB) as b_:
                        for hq in range(HEADS // HQ):
                            i = hq % 2
                            dve.wait_ge(q_ps, FROM + b_ * (HEADS // HQ) + hq + 1)
                            if hq >= 2:
                                dve.wait_ge(masked, FROM + b_ * (HEADS // HQ) + hq - 1)
                            else:
                                dve.wait_ge(masked, FROM + b_ * (HEADS // HQ))
                            for j in range(TPB):
                                keys = k_tok[:, bass.ds(b_ * (TPB * HEADS) + j * HEADS + hq * HQ, HQ)]
                                nc.vector.tensor_tensor(
                                    mask[i][j][:, :].rearrange("p (h t) -> p h t", t=T),
                                    psq[i][:, :].rearrange("p (h t) -> p h t", t=T),
                                    keys.unsqueeze(2).broadcast_to([P, HQ, T]), ALU.is_ge).then_inc(mask_ready, 1)
                        c = Chain(dve, batch_self, b_ * steps)
                        dve.wait_ge(masked, FROM + (b_ + 1) * (HEADS // HQ))
                        for u in range(TPB):
                            for half in range(2):
                                o = (u * HEADS + half * HALF) * VC
                                last = nc.vector.tensor_reduce(
                                    sums[:, o:o + HALF * VC].rearrange("p (h r) -> p h r", r=VC),
                                    pso[u * 2 + half][:, 0:HALF * HV].rearrange("p (h s r) -> p h r s", s=PARTS, r=VC),
                                    axis=AX.X, op=ALU.add)
                        last.then_inc(sums_out, 1)
                        dve.wait_ge(sums_out, FROM + b_ + 1)
                        S = sums[:, :].rearrange("p (h r) -> p h r", r=VC)
                        q = at(q_tok, b_ * (TPB * HEADS), TPB * HEADS)
                        q_b = q.unsqueeze(2).broadcast_to([P, TPB * HEADS, HD])
                        num3 = num[:, :].rearrange("p (h r) -> p h r", r=HD)
                        c.mark(nc.vector.tensor_tensor(n1[:, :], S[:, :, 2 * HD], q, ALU.mult))
                        c.mark(nc.vector.tensor_scalar(n2[:, :], q, float(T), None, ALU.mult))
                        c.link(nc.vector.tensor_tensor(num3, S[:, :, 0:HD], q_b, ALU.mult))
                        c.mark(nc.vector.tensor_tensor(n1[:, :], n1[:, :], S[:, :, 2 * HD + 1], ALU.subtract))
                        ks = at(k_sum, b_ * HEADS, HEADS).unsqueeze(1).broadcast_to([P, TPB, HEADS])
                        c.mark(nc.vector.tensor_tensor(n2[:, :].rearrange("p (u h) -> p u h", h=HEADS),
                                                       n2[:, :].rearrange("p (u h) -> p u h", h=HEADS), ks, ALU.subtract))
                        c.link(nc.vector.tensor_tensor(num3, num3, S[:, :, HD:2 * HD], ALU.subtract))
                        c.link(nc.vector.scalar_tensor_tensor(n1[:, :], n1[:, :], 2.0, n2[:, :], ALU.mult, ALU.subtract))
                        c.link(nc.vector.tensor_scalar(n1[:, :], n1[:, :], 1e-4, None, ALU.max))
                        c.link(nc.vector.reciprocal(n1[:, :], n1[:, :]))
                        c.link(nc.vector.tensor_scalar(n1[:, :], n1[:, :], 2.0, None, ALU.mult))
                        c.link(nc.vector.tensor_tensor(at(y_tok, b_ * T, T).rearrange("p (h r) -> p h r", r=HD), num3,
                                                       n1[:, :].unsqueeze(2).broadcast_to([P, TPB * HEADS, HD]), ALU.mult))
                        assert c.n == steps, c.n

                @block.scalar
                def _(act):
                    act.wait_ge(var_ready, FROM + 1)
                    nc.scalar.activation(pvar["q"][:, :], pvar["q"][:, :], ACT.Sqrt, bias=eps_std[0:PR, :],
                                         scale=0.5 / T).then_inc(std_ready, 1)
                    with act.Fori(0, NB) as b_:
                        act.wait_ge(qk_ps, FROM + b_ + 1)
                        for x, dst in enumerate((q_tok, k_tok)):
                            last = nc.scalar.activation(
                                at(dst, b_ * (TPB * HEADS), TPB * HEADS).rearrange("p (u h) -> p u h", h=HEADS),
                                pso[0][:, x * TPB * P:(x + 1) * TPB * P].rearrange(
                                    "p (u h) -> p u h", h=P)[:, :, 0:HEADS], ACT.Copy)
                        last.then_inc(qk_sb, 1)
                        act.wait_ge(ksum_ps, FROM + b_ + 1)
                        nc.scalar.activation(at(k_sum, b_ * HEADS, HEADS), pso[1][:, 0:HEADS],
                                             ACT.Copy).then_inc(ksum_sb, 1)
                    with act.Fori(0, NB // 2) as b2_:
                        for u in range(2):
                            act.wait_ge(vals_used, FROM + b2_ * 2 + u)
                            for j in range(TPB):
                                tile = b2_ * (2 * TPB) + u * TPB + j
                                part = vals[u][:, j * HEADS * HV:(j + 1) * HEADS * HV].rearrange(
                                    "p (h s r) -> p h s r", s=PARTS, r=VC)
                                act.wait_ge(cols_ready, FROM + tile + 1)
                                nc.scalar.activation(part[:, :, 0, :], cols[:, :].rearrange(
                                    "p (h r) -> p h r", r=VC), ACT.Copy).then_inc(hi_ready, 1)
                                act.wait_ge(rest_ready, FROM + tile + 1)
                                nc.scalar.activation(part[:, :, 1, :], rest[:, :].rearrange(
                                    "p (h r) -> p h r", r=VC), ACT.Copy).then_inc(mid_ready, 1)

                @block.gpsimd
                def _(pool):
                    nc.gpsimd.memset(qn[PR:P, :], 0.0).then_inc(rows_cleared, 1)
                    nc.gpsimd.memset(kn[PR:P, :], 0.0).then_inc(rows_cleared, 1)
                    nc.gpsimd.memset(q_parts[PR:P, :].bitcast(F32), 0.0).then_inc(rows_cleared, 1)
                    pool.wait_ge(rows_cleared, FROM + 3)
                    nc.gpsimd.memset(pick[:, :].bitcast(F32), 0.0).then_inc(pick_made, 1)
                    pool.wait_ge(pick_made, FROM + 1)
                    for r in range(2):
                        dst = pick[r * HR:r * HR + HR, :].rearrange("p (h t) -> p h t", t=P)
                        nc.gpsimd.affine_select(out=dst, in_=pick[r * HR:r * HR + HR, :].bitcast(F32).rearrange(
                            "p (h t) -> p h t", t=P), compare_op=ALU.not_equal, fill=1.0, base=0,
                            pattern=[[-1, HEADS], [0, P]], channel_multiplier=1).then_inc(pick_made, 1)
                    pool.wait_ge(pick_made, FROM + 3)
                    c3 = cols[:, :].rearrange("p (h r) -> p h r", r=VC)
                    nc.gpsimd.memset(c3[:, :, 2 * HD:2 * HD + 1], 1.0)
                    r3 = rest[:, :].rearrange("p (h r) -> p h r", r=VC)
                    with pool.Fori(0, NB // 2) as b2_:
                        for u in range(2):
                            for j in range(TPB):
                                tile = b2_ * (2 * TPB) + u * TPB + j
                                part = vals[u][:, j * HEADS * HV:(j + 1) * HEADS * HV].rearrange(
                                    "p (h s r) -> p h s r", s=PARTS, r=VC)
                                pool.wait_ge(qk_sb, FROM + b2_ * 2 + u + 1)
                                pool.wait_ge(hi_ready, FROM + tile)
                                v3 = at(v_tok, tile * P, P).rearrange("p (h r) -> p h r", r=HD)
                                k2 = at(k_tok, tile * HEADS, HEADS)
                                nc.gpsimd.tensor_copy(c3[:, :, 0:HD], v3)
                                nc.gpsimd.tensor_tensor(c3[:, :, HD:2 * HD], v3,
                                                        k2.unsqueeze(2).broadcast_to([P, HEADS, HD]), ALU.mult)
                                nc.gpsimd.tensor_copy(c3[:, :, 2 * HD + 1], k2).then_inc(cols_ready, 1)
                                pool.wait_ge(hi_ready, FROM + tile + 1)
                                pool.wait_ge(mid_ready, FROM + tile)
                                nc.gpsimd.tensor_tensor(r3, c3, part[:, :, 0, :], ALU.subtract).then_inc(rest_ready, 1)
                                pool.wait_ge(mid_ready, FROM + tile + 1)
                                ins = nc.gpsimd.tensor_tensor(part[:, :, 2, :], r3, part[:, :, 1, :], ALU.subtract)
                            ins.then_inc(vals_ready, 1)

                @block.tensor
                def _(pe):
                    pe.wait_ge(rows_cleared, FROM + 3)
                    with pe.Fori(0, NB) as b_:
                        pe.wait_ge(qk_rows, FROM + b_ + 1)
                        pe.wait_ge(qk_sb, FROM + b_)
                        for x, src in enumerate((qn, kn)):
                            for t in range(TPB):
                                o = (x * TPB + t) * P
                                last = nc.tensor.transpose(pso[0][:, o:o + P], src[:, t * P:(t + 1) * P],
                                                           ident[:, :])
                        last.then_inc(qk_ps, 1)
                        pe.wait_ge(qk_sb, FROM + b_ + 1)
                        pe.wait_ge(ksum_sb, FROM + b_)
                        for t in range(TPB):
                            last = nc.tensor.matmul(pso[1][:, 0:HEADS], ones[:, :],
                                                    at(k_tok, b_ * (TPB * HEADS) + t * HEADS, HEADS),
                                                    start=(t == 0), stop=(t == TPB - 1))
                        last.then_inc(ksum_ps, 1)
                    pe.wait_ge(ksum_sb, FROM + NB)
                    pe.wait_ge(pick_made, FROM + 3)
                    pe.wait_ge(prep, FROM + NB * 4)

                    def spread_q(b_, hq, n):
                        i = hq % 2
                        for h in range(HQ):
                            last = nc.tensor.matmul(psq[i][:, h * T:(h + 1) * T],
                                                    pick[:, (hq * HQ + h) * P:(hq * HQ + h + 1) * P],
                                                    q_parts[:, bass.ds(b_ * T, T)], start=True, stop=True)
                        last.then_inc(q_ps, 1)

                    QS = HEADS // HQ
                    with pe.Fori(0, NB // 2) as b2_:
                        for u in range(2):
                            b_ = b2_ * 2 + u
                            for hq in range(QS):
                                i = hq % 2
                                if hq == 0:
                                    pe.wait_ge(mask_ready, FROM + b_ * (QS * TPB))
                                    spread_q(b_, 0, 0)
                                    spread_q(b_, 1, 0)
                                elif hq < QS - 1:
                                    pe.wait_ge(mask_ready, FROM + (b_ * QS + hq) * TPB)
                                    spread_q(b_, hq + 1, 0)
                                pe.wait_ge(mask_ready, FROM + (b_ * QS + hq + 1) * TPB)
                                if hq == 0:
                                    pe.wait_ge(vals_ready, FROM + b_ + 1)
                                    pe.wait_ge(sums_out, FROM + b_)
                                for h in range(HQ):
                                    head = hq * HQ + h
                                    o = (head % HALF) * HV
                                    for ic in range(TPB):
                                        for j in range(TPB):
                                            vo = (j * HEADS + head) * HV
                                            last = nc.tensor.matmul(
                                                pso[ic * 2 + head // HALF][:, o:o + HV],
                                                mask[i][j][:, h * T + ic * P:h * T + ic * P + P],
                                                vals[u][:, vo:vo + HV], start=(j == 0), stop=(j == TPB - 1))
                                last.then_inc(masked, 1)
                            pe.sem_inc(vals_used, 1)


def experts(nc, a, env, layer):
    x_tok, y_tok, h_tok, ident = env["x_tok"], env["y_tok"], env["h_tok"], env["ident"]
    gated = layer == 0
    E, K = ((E0, K0), (E1, K1))[layer]
    CH = 1 if gated else CH1
    pre = f"e{layer}_"
    LW = E + 8
    outside = -1.0 if gated else OUTSIDE
    if gated:
        UPS = [("gate0", E * P), ("up0", E * P), ("sgate0", SH0 * P), ("sup0", SH0 * P)]
        DOWNS = [("down0", E * P), ("sdown0", SH0 * P)]
    else:
        UPS = [("ew1", E * CH * P), ("sw1", CH * P)]
        DOWNS = [("ew2", E * CH * P), ("sw2", CH * P)]
    phase = ExitStack()
    with phase:
        def sb(name, cols, dt=F32, rows=P):
            return phase.enter_context(nc.sbuf_tensor(pre + name, [rows, cols], dt))

        h_hi, h_lo = sb("h_hi", N, F32R), sb("h_lo", N, F32R)
        w_hi = {n: sb(n + "_hi", c, F32R) for n, c in UPS}
        w_lo = {n: sb(n + "_lo", c, F32R) for n, c in UPS}
        w_down = {n: sb(n, c) for n, c in DOWNS}
        gates = sb("gates", TILES * E)

        with ExitStack() as s:
            def tb(name, cols, dt=F32, rows=P):
                return s.enter_context(nc.sbuf_tensor(pre + name, [rows, cols], dt))
            sem = lambda n: env["semaphore"](pre + n)
            ps = [s.enter_context(nc.psum_tensor(f"{pre}ps{i}", [P, GW], F32)) for i in range(4)]
            router = tb("router", E)
            bias = tb("bias", E)
            h_fm = [tb(f"h_fm{i}", GW) for i in range(2)]
            logits = tb("logits", TILES * LW)
            left = tb("left", TILES * LW)
            best, chosen = tb("best", TILES * 8), tb("chosen", TILES * 8)
            total = tb("total", TILES)
            SC = 512
            stage = [tb(f"stage{i}", SC) for i in range(2)]
            pieces = [(n, o) for n, c in UPS for o in range(0, c, SC)]
            staged = [sem("staged0"), sem("staged1")]
            small, downs = sem("small"), sem("downs")
            stats_done, self_done, var_ready, std_ready = map(
                sem, ("stats_done", "dve_done", "var_ready", "std_ready"))
            rows_ready, fm_ps, fm_sb, split, logit_ps, logit_sb = map(
                sem, ("rows_ready", "fm_ps", "fm_sb", "split", "logit_ps", "logit_sb"))
            hi_made, lo_made = sem("hi_made"), sem("lo_made")
            shifted, exped = sem("shifted"), sem("exped")
            L = logits[:, :].rearrange("p (t e) -> p t e", e=LW)
            R = left[:, :].rearrange("p (t e) -> p t e", e=LW)
            B = best[:, :].rearrange("p (t e) -> p t e", e=8)
            C = chosen[:, :].rearrange("p (t e) -> p t e", e=8)
            G = gates[:, :].rearrange("p (t e) -> p t e", e=E)
            with nc.Block() as block:
                @block.sync
                def _(sp):
                    sp.dma_start(router[:, :], a["router" if gated else "gate_w1"]).then_inc(small, 16)
                    if gated:
                        sp.dma_start(bias[:, :], a["router_bias"].partition_broadcast(P)).then_inc(small, 16)
                    for i, (n, o) in enumerate(pieces):
                        if i >= 2:
                            sp.wait_ge(lo_made, FROM + i - 1)
                        sp.dma_start(stage[i % 2][:, :], a[n][:, o:o + SC]).then_inc(staged[i % 2], 16)
                    for n in w_down:
                        sp.dma_start(w_down[n][:, :], a[n]).then_inc(downs, 16)
                    sp.wait_ge(downs, FROM + 16 * len(w_down))

                @block.gpsimd
                def _(pool):
                    for i, (n, o) in enumerate(pieces):
                        pool.wait_ge(staged[i % 2], FROM + 16 * (i // 2 + 1))
                        nc.gpsimd.tensor_copy(w_hi[n][:, o:o + SC], stage[i % 2][:, :]).then_inc(hi_made, 1)
                        pool.wait_ge(hi_made, FROM + i + 1)
                        nc.gpsimd.tensor_tensor(w_lo[n][:, o:o + SC], stage[i % 2][:, :],
                                                w_hi[n][:, o:o + SC].bitcast(F32), ALU.subtract).then_inc(lo_made, 1)

                @block.tensor
                def _(pe):
                    for g in range(GROUPS + 1):
                        if g < GROUPS:
                            pe.wait_ge(rows_ready, FROM + g + 1)
                            if g >= 2:
                                pe.wait_ge(fm_sb, FROM + g - 1)
                            for t in range(TPG):
                                o = (g * TPG + t) * P
                                last = nc.tensor.transpose(ps[g % 2][:, t * P:(t + 1) * P],
                                                           h_tok[:, o:o + P], ident[:, :])
                            last.then_inc(fm_ps, 1)
                        if g:
                            i = g - 1
                            if i == 0:
                                pe.wait_ge(small, FROM + (32 if gated else 16))
                            pe.wait_ge(fm_sb, FROM + i + 1)
                            if i >= 2:
                                pe.wait_ge(logit_sb, FROM + i - 1)
                            for t in range(TPG):
                                last = nc.tensor.matmul(ps[2 + i % 2][:, t * E:(t + 1) * E],
                                                        h_fm[i % 2][:, t * P:(t + 1) * P], router[:, :],
                                                        start=True, stop=True)
                            last.then_inc(logit_ps, 1)

                @block.scalar
                def _(act):
                    env["norm_act"](act, var_ready, std_ready)
                    for g in range(GROUPS):
                        act.wait_ge(fm_ps, FROM + g + 1)
                        if g >= 2:
                            act.wait_ge(split, FROM + g - 1)
                            act.wait_ge(logit_ps, FROM + g - 1)
                        nc.scalar.activation(h_fm[g % 2][:, :], ps[g % 2][:, :], ACT.Copy).then_inc(fm_sb, 1)
                    act.wait_ge(shifted, FROM + 1)
                    dst = L[:, :, 0:E] if gated else G
                    nc.scalar.activation(dst, L[:, :, 0:E] if gated else G, ACT.Exp).then_inc(exped, 1)

                @block.vector
                def _(dve):
                    c = Chain(dve, self_done)
                    env["norm_dve"](dve, c, x_tok, stats_done, var_ready, std_ready)
                    env["norm_rows"](dve, x_tok, h_tok, rows_ready)
                    c.mark(nc.vector.memset(L[:, :, E:LW], outside))
                    c.link(nc.vector.memset(chosen[:, :], outside))
                    dve.wait_ge(small, FROM + (32 if gated else 16))
                    for g in range(GROUPS):
                        dve.wait_ge(fm_sb, FROM + g + 1)
                        o = g * GW
                        c.link(nc.vector.tensor_copy(h_hi[:, o:o + GW], h_fm[g % 2][:, :]))
                        nc.vector.tensor_tensor(h_lo[:, o:o + GW], h_fm[g % 2][:, :],
                                                h_hi[:, o:o + GW].bitcast(F32), ALU.subtract).then_inc(split, 1)
                        dve.wait_ge(logit_ps, FROM + g + 1)
                        src = ps[2 + g % 2][:, 0:TPG * E].rearrange("p (t e) -> p t e", e=E)
                        dst = L[:, g * TPG:(g + 1) * TPG, 0:E]
                        if gated:
                            ins = nc.vector.tensor_tensor(dst, src, bias[:, :].unsqueeze(1).broadcast_to(
                                [P, TPG, E]), ALU.add)
                        else:
                            ins = nc.vector.tensor_copy(dst, src)
                        ins.then_inc(logit_sb, 1)
                    dve.wait_ge(logit_sb, FROM + GROUPS)
                    for t in range(TILES):
                        c.mark(nc.vector.max(B[:, t], L[:, t, 0:E]))
                    c.wait()
                    first = B[:, :, 0:1].broadcast_to([P, TILES, E])
                    if gated:
                        nc.vector.tensor_tensor(L[:, :, 0:E], L[:, :, 0:E], first, ALU.subtract).then_inc(shifted, 1)
                        dve.wait_ge(exped, FROM + 1)
                        c.link(nc.vector.tensor_reduce(total[:, :], L[:, :, 0:E], axis=AX.X, op=ALU.add))
                        c.link(nc.vector.reciprocal(total[:, :], total[:, :]))
                        c.link(nc.vector.tensor_tensor(L[:, :, 0:E], L[:, :, 0:E], total[:, :].unsqueeze(
                            2).broadcast_to([P, TILES, E]), ALU.mult))
                        for t in range(TILES):
                            c.mark(nc.vector.max(B[:, t], L[:, t, 0:E]))
                        c.wait()
                    else:
                        nc.vector.tensor_tensor(G, L[:, :, 0:E], first, ALU.subtract).then_inc(shifted, 1)
                    c.link(nc.vector.tensor_copy(C[:, :, 0:K], B[:, :, 0:K]))
                    for t in range(TILES):
                        c.mark(nc.vector.match_replace(R[:, t], C[:, t], L[:, t], 0.0 if gated else -OUTSIDE))
                    c.wait()
                    if gated:
                        c.mark(nc.vector.tensor_tensor(G, L[:, :, 0:E], R[:, :, 0:E], ALU.subtract))
                        c.link(nc.vector.tensor_reduce(total[:, :], B[:, :, 0:K], axis=AX.X, op=ALU.add))
                        c.link(nc.vector.tensor_scalar(total[:, :], total[:, :], 1e-12, None, ALU.max))
                    else:
                        c.link(nc.vector.tensor_tensor(R[:, :, 0:E], L[:, :, 0:E], R[:, :, 0:E], ALU.not_equal))
                        dve.wait_ge(exped, FROM + 1)
                        c.link(nc.vector.tensor_tensor(G, G, R[:, :, 0:E], ALU.mult))
                        c.link(nc.vector.tensor_reduce(total[:, :], G, axis=AX.X, op=ALU.add))
                    c.link(nc.vector.reciprocal(total[:, :], total[:, :]))
                    nc.vector.tensor_tensor(G, G, total[:, :].unsqueeze(2).broadcast_to([P, TILES, E]), ALU.mult)

        with ExitStack() as s:
            def tb(name, cols, dt=F32, rows=P):
                return s.enter_context(nc.sbuf_tensor(pre + name, [rows, cols], dt))
            sem = lambda n: env["semaphore"](pre + n)
            NU = 3
            ps_up = [s.enter_context(nc.psum_tensor(f"{pre}up{i}", [P, GW], F32)) for i in range(NU)]
            ps_gate = [s.enter_context(nc.psum_tensor(f"{pre}gate{i}", [P, GW], F32)) for i in range(NU)] if gated else ps_up
            ps_y = [s.enter_context(nc.psum_tensor(f"{pre}y{i}", [P, GW], F32)) for i in range(2)]
            silu = [tb(f"silu{i}", GW) for i in range(NU)]
            hidden = [tb(f"hidden{i}", GW) for i in range(NU)] if gated else silu
            acc = tb("acc", GW)
            g_now = tb("g_now", TPG * E)
            gate_ps, up_ps, silu_ready, hidden_ready, down_ps, added, acc_self, acc_out = map(
                sem, ("gate_ps", "up_ps", "silu_ready", "hidden_ready", "down_ps", "added", "acc_self", "acc_out"))
            if gated:
                units = [("s", i) for i in range(SH0)] + [("e", i) for i in range(E)]
            else:
                units = [("s", 0)] + [("e", i) for i in range(E)]
            U = len(units)
            steps = U * CH
            hidden_sem = hidden_ready if gated else silu_ready

            def first_weights(kind, i, c):
                if gated:
                    return ("sgate0", "sup0", i * P) if kind == "s" else ("gate0", "up0", i * P)
                return (None, "sw1", c * P) if kind == "s" else (None, "ew1", (i * CH + c) * P)

            def second_weights(kind, i, c):
                if gated:
                    return w_down["sdown0" if kind == "s" else "down0"][:, i * P:(i + 1) * P]
                o = (c if kind == "s" else i * CH + c) * P
                return w_down["sw2" if kind == "s" else "ew2"][:, o:o + P]

            with nc.Block() as block:
                @block.tensor
                def _(pe):
                    with pe.Fori(0, GROUPS) as g:
                        hi, lo = at(h_hi, g * GW, GW), at(h_lo, g * GW, GW)

                        def product(bank, name, o, done):
                            wh, wl = w_hi[name][:, o:o + P], w_lo[name][:, o:o + P]
                            nc.tensor.matmul(bank[:, :], wl, hi, start=True, stop=False)
                            nc.tensor.matmul(bank[:, :], wh, lo, start=False, stop=False)
                            nc.tensor.matmul(bank[:, :], wh, hi, start=False, stop=True).then_inc(done, 1)

                        for n in range(steps + 1):
                            if n < steps:
                                kind, i = units[n // CH]
                                gate, up, o = first_weights(kind, i, n % CH)
                                before = g * steps + (n - NU + 1 if n >= NU - 1 else 0)
                                if gate:
                                    pe.wait_ge(silu_ready, FROM + before)
                                    product(ps_gate[n % NU], gate, o, gate_ps)
                                pe.wait_ge(hidden_sem, FROM + before)
                                product(ps_up[n % NU], up, o, up_ps)
                            if n:
                                m = n - 1
                                (kind, i), c = units[m // CH], m % CH
                                pe.wait_ge(hidden_sem, FROM + g * steps + m + 1)
                                if c == 0:
                                    u = m // CH
                                    pe.wait_ge(added, FROM + (g * U + (u - 1 if u else 0)))
                                for t in range(TPG):
                                    last = nc.tensor.matmul(
                                        ps_y[m // CH % 2][:, t * P:(t + 1) * P],
                                        hidden[m % NU][:, t * P:(t + 1) * P], second_weights(kind, i, c),
                                        start=(c == 0 and t == 0), stop=(c == CH - 1), skip_group_check=True)
                                last.then_inc(down_ps, 1)

                @block.scalar
                def _(act):
                    with act.Fori(0, GROUPS) as g:
                        for n in range(steps):
                            if gated:
                                act.wait_ge(gate_ps, FROM + g * steps + n + 1)
                                before = g * steps + (n - NU + 1 if n >= NU - 1 else 0)
                                act.wait_ge(hidden_ready, FROM + before)
                                nc.scalar.activation(silu[n % NU][:, :], ps_gate[n % NU][:, :],
                                                     ACT.Silu).then_inc(silu_ready, 1)
                            else:
                                act.wait_ge(up_ps, FROM + g * steps + n + 1)
                                act.wait_ge(down_ps, FROM + g * steps + max(n - NU + 1, 0))
                                nc.scalar.activation(silu[n % NU][:, :], ps_up[n % NU][:, :],
                                                     ACT.Silu).then_inc(silu_ready, 1)

                @block.vector
                def _(dve):
                    with dve.Fori(0, GROUPS) as g:
                        c = Chain(dve, acc_self, g)
                        c.link(nc.vector.tensor_copy(g_now[:, :], at(gates, g * (TPG * E), TPG * E)))
                        for n in range(U + 1):
                            if gated and n < U:
                                dve.wait_ge(silu_ready, FROM + g * steps + n + 1)
                                dve.wait_ge(up_ps, FROM + g * steps + n + 1)
                                dve.wait_ge(down_ps, FROM + g * steps + max(n - NU + 1, 0))
                                nc.vector.tensor_tensor(hidden[n % NU][:, :], ps_up[n % NU][:, :],
                                                        silu[n % NU][:, :], ALU.mult).then_inc(hidden_ready, 1)
                            if n:
                                u = n - 1
                                kind, i = units[u]
                                y = ps_y[u % 2]
                                dve.wait_ge(down_ps, FROM + g * steps + (u + 1) * CH)
                                if u == 0:
                                    dve.wait_ge(acc_out, FROM + g)
                                    last = nc.vector.tensor_copy(acc[:, :], y[:, :])
                                elif kind == "s":
                                    last = nc.vector.tensor_tensor(acc[:, :], y[:, :], acc[:, :], ALU.add)
                                else:
                                    for t in range(TPG):
                                        cols = slice(t * P, (t + 1) * P)
                                        last = nc.vector.scalar_tensor_tensor(
                                            acc[:, cols], y[:, cols], g_now[:, t * E + i:t * E + i + 1],
                                            acc[:, cols], ALU.mult, ALU.add)
                                last.then_inc(added, 1)
                                dve.wait_ge(added, FROM + g * U + u + 1)

                @block.gpsimd
                def _(pool):
                    with pool.Fori(0, GROUPS) as g:
                        pool.wait_ge(added, FROM + (g + 1) * U)
                        nc.gpsimd.tensor_copy(at(y_tok, g * GW, GW), acc[:, :]).then_inc(acc_out, 1)


def rwkv(nc, a, env):
    x_tok, y_tok, h_tok, ident = env["x_tok"], env["y_tok"], env["h_tok"], env["ident"]
    W1T = T + 1
    phase = ExitStack()
    with phase:
        def sb(name, cols, dt=F32, rows=P):
            return phase.enter_context(nc.sbuf_tensor("c_" + name, [rows, cols], dt))

        mats = {n: sb(n, P) for n in ("att_Wk", "att_Wv", "att_Wr", "att_Wo", "ffn_Wr")}
        mats["ffn_Wk"] = sb("ffn_Wk", CH_RWKV * P)
        mats["ffn_Wv"] = sb("ffn_Wv", CH_RWKV * P)
        NVEC = ("ln1_g", "ln1_b", "ln2_g", "ln2_b", "time_decay", "time_first", "time_mix_k", "time_mix_v",
                "time_mix_r", "cm_k", "cm_r")
        vec = {n: sb(n, 1) for n in NVEC}
        rest_of = {n: sb(n + "_rest", 1) for n in ("time_mix_k", "time_mix_v", "time_mix_r", "cm_k", "cm_r")}
        decay = sb("decay", 1)

        def load_norm_transpose(tag, src, to_h, gname, bname, dst, first):
            with ExitStack() as s:
                sem = lambda n: env["semaphore"](tag + n)
                ps = [s.enter_context(nc.psum_tensor(f"{tag}ps{i}", [P, GW], F32)) for i in range(2)]
                loaded, derived = sem("loaded"), sem("derived")
                sems = [tuple(map(sem, (f"stats{i}", f"dve{i}", f"var{i}", f"std{i}", f"rows{i}"))) for i in range(2)]
                fm_ps, fm_sb = sem("fm_ps"), sem("fm_sb")
                NL = 16 * (len(mats) + len(vec))
                with nc.Block() as block:
                    if first:
                        @block.sync
                        def _(sp):
                            for n in vec:
                                sp.dma_start(vec[n][:, :], a[n]).then_inc(loaded, 16)
                            for n in mats:
                                sp.dma_start(mats[n][:, :], a[n]).then_inc(loaded, 16)
                            sp.wait_ge(loaded, FROM + NL)

                    @block.vector
                    def _(dve):
                        d3 = dst[:, :].rearrange("p (b t) -> p b t", t=W1T)
                        nc.vector.memset(d3[:, :, 0:1], 0.0)
                        if to_h:
                            st, own, var, std, rows = sems[0]
                            env["norm_dve"](dve, Chain(dve, own), src, st, var, std)
                            env["norm_rows"](dve, src, h_tok, rows)
                            dve.wait_ge(rows, FROM + GROUPS)
                        st, own, var, std, rows = sems[1]
                        env["norm_dve"](dve, Chain(dve, own), h_tok, st, var, std)
                        env["norm_rows"](dve, h_tok, y_tok, rows)
                        if first:
                            dve.wait_ge(loaded, FROM + NL)
                            for n in rest_of:
                                nc.vector.tensor_scalar(rest_of[n][:, :], vec[n][:, :], -1.0, 1.0, ALU.mult, ALU.add)
                            dve.wait_ge(derived, FROM + 1)
                            nc.vector.tensor_scalar(decay[:, :], decay[:, :], -1.0, None, ALU.mult)

                    @block.scalar
                    def _(act):
                        if first:
                            act.wait_ge(loaded, FROM + NL)
                            nc.scalar.activation(decay[:, :], vec["time_decay"][:, :], ACT.Exp).then_inc(derived, 1)
                        if to_h:
                            env["norm_act"](act, sems[0][2], sems[0][3])
                        env["norm_act"](act, sems[1][2], sems[1][3])
                        for g in range(GROUPS):
                            act.wait_ge(fm_ps, FROM + g + 1)
                            o = g * BPG * W1T
                            nc.scalar.activation(
                                dst[:, o:o + BPG * W1T].rearrange("p (b t) -> p b t", t=W1T)[:, :, 1:W1T],
                                ps[g % 2][:, :].rearrange("p (b t) -> p b t", t=T), ACT.Identity,
                                bias=vec[bname][:, :], scale=vec[gname][:, :]).then_inc(fm_sb, 1)

                    @block.tensor
                    def _(pe):
                        env["transposes"](pe, y_tok, ps, sems[1][4], fm_ps, fm_sb)

        def mixed(c, src, g, name, tmp, dst):
            s3 = at(src, g * (BPG * W1T), BPG * W1T).rearrange("p (b t) -> p b t", t=W1T)
            t3 = tmp[:, :].rearrange("p (b t) -> p b t", t=T)
            d3 = dst[:, :].rearrange("p (b t) -> p b t", t=T)
            c.link(nc.vector.tensor_scalar(t3, s3[:, :, 0:T], rest_of[name][:, :], None, ALU.mult))
            return nc.vector.scalar_tensor_tensor(d3, s3[:, :, 1:W1T], vec[name][:, :], t3, ALU.mult, ALU.add)

        with ExitStack() as rkv:
            k_all, v_all, r_all = (rkv.enter_context(nc.sbuf_tensor(n, [P, N], F32)) for n in ("k_all", "v_all", "r_all"))

            with ExitStack() as s:
                def tb(name, cols, dt=F32, rows=P):
                    return s.enter_context(nc.sbuf_tensor(name, [rows, cols], dt))
                xa = tb("xa", NB * W1T)
                load_norm_transpose("c1_", x_tok, True, "ln1_g", "ln1_b", xa, True)
                sem = lambda n: env["semaphore"]("c2_" + n)
                names = ("k", "v", "r")
                mix = {n: tb("mix_" + n, GW) for n in names}
                tmp = {n: tb("mix_tmp_" + n, GW) for n in names}
                ps = {n: [s.enter_context(nc.psum_tensor(f"c2_ps_{n}{i}", [P, GW], F32)) for i in range(2)] for n in names}
                mix_ready = {n: sem("mix_" + n) for n in names}
                out_ps = {n: sem("ps_" + n) for n in names}
                out_sb = {n: sem("sb_" + n) for n in names}
                own = sem("dve_done")
                with nc.Block() as block:
                    @block.vector
                    def _(dve):
                        with dve.Fori(0, GROUPS) as g:
                            c = Chain(dve, own, g * 3)
                            for n in names:
                                dve.wait_ge(out_ps[n], FROM + g)
                                mixed(c, xa, g, "time_mix_" + n, tmp[n], mix[n]).then_inc(mix_ready[n], 1)

                    @block.tensor
                    def _(pe):
                        with pe.Fori(0, GROUPS // 2) as g2:
                            for u in range(2):
                                for n in names:
                                    pe.wait_ge(mix_ready[n], FROM + g2 * 2 + u + 1)
                                    pe.wait_ge(out_sb[n], FROM + g2 * 2)
                                    nc.tensor.matmul(ps[n][u][:, :], mats["att_W" + n][:, :], mix[n][:, :],
                                                     start=True, stop=True).then_inc(out_ps[n], 1)

                    @block.scalar
                    def _(act):
                        with act.Fori(0, GROUPS // 2) as g2:
                            for u in range(2):
                                for n, dst in zip(names, (k_all, v_all, r_all)):
                                    act.wait_ge(out_ps[n], FROM + g2 * 2 + u + 1)
                                    nc.scalar.activation(at(dst, g2 * (2 * GW) + u * GW, GW), ps[n][u][:, :],
                                                         ACT.Sigmoid if n == "r" else ACT.Copy).then_inc(out_sb[n], 1)

            with ExitStack() as s:
                def tb(name, cols, dt=F32, rows=P):
                    return s.enter_context(nc.sbuf_tensor("s_" + name, [rows, cols], dt))
                sem = lambda n: env["semaphore"]("c3_" + n)
                w_row = tb("w_row", T)
                peak = tb("peak", BPG * W1T)
                peak_out = tb("peak_out", GW)
                KINDS = 4
                ex = tb("ex", GROUPS * KINDS * GW)
                new_v = [tb(f"new_v{i}", GW) for i in range(2)]
                out_v = [tb(f"out_v{i}", GW) for i in range(2)]
                a_st, b_st = tb("a_st", BPG * W1T), tb("b_st", BPG * W1T)
                num, den = tb("num", GW), tb("den", GW)
                wkv = tb("wkv", GW)
                ps = [s.enter_context(nc.psum_tensor(f"c3_ps{i}", [P, GW], F32)) for i in range(1)]
                own1, own2, diffs, exped, vs_ready, vs_used, wkv_ready, wo_ps, wo_sb = map(
                    sem, ("own1", "own2", "diffs", "exped", "vs_ready", "vs_used", "wkv_ready", "wo_ps", "wo_sb"))

                def b3(x, n=T):
                    return x.rearrange("p (b t) -> p b t", t=n)

                with nc.Block() as block:
                    @block.vector
                    def _(dve):
                        own0 = own1
                        c = Chain(dve, own0)
                        c.mark(nc.vector.memset(w_row[:, :], 0.0))
                        c.mark(nc.vector.memset(b3(peak[:, :], W1T)[:, :, 0:1], NEVER))
                        c.mark(nc.vector.memset(b3(a_st[:, :], W1T)[:, :, 0:1], 0.0))
                        c.link(nc.vector.memset(b3(b_st[:, :], W1T)[:, :, 0:1], 0.0))
                        c.link(nc.vector.tensor_scalar(w_row[:, :], w_row[:, :], decay[:, :], None, ALU.add))
                        start, steps = c.n, 3
                        u_ = vec["time_first"][:, :]
                        with dve.Fori(0, GROUPS) as g:
                            c = Chain(dve, own1, start + g * steps)
                            dve.wait_ge(diffs, FROM + g)
                            for i in range(BPG):
                                c.mark(nc.vector.tensor_tensor_scan(
                                    peak[:, i * W1T + 1:(i + 1) * W1T], w_row[:, :], at(k_all, g * GW + i * T, T),
                                    NEVER, ALU.add, ALU.max))
                            k3 = b3(at(k_all, g * GW, GW))
                            was, now = b3(peak[:, :], W1T)[:, :, 0:T], b3(peak[:, :], W1T)[:, :, 1:W1T]
                            c.wait()
                            e = [b3(at(ex, g * (KINDS * GW) + i * GW, GW)) for i in range(KINDS)]
                            c.link(nc.vector.scalar_tensor_tensor(b3(peak_out[:, :]), k3, u_, was, ALU.add, ALU.max))
                            nc.vector.scalar_tensor_tensor(e[0], was, decay[:, :], now, ALU.add, ALU.subtract)
                            nc.vector.tensor_tensor(e[1], k3, now, ALU.subtract)
                            nc.vector.tensor_tensor(e[2], was, b3(peak_out[:, :]), ALU.subtract)
                            nc.vector.scalar_tensor_tensor(e[3], k3, u_, b3(peak_out[:, :]), ALU.add,
                                                           ALU.subtract).then_inc(diffs, 1)
                        steps = 7
                        with dve.Fori(0, GROUPS // 2) as g2:
                            for u in range(2):
                                g = g2 * 2 + u
                                c = Chain(dve, own2, g * steps)
                                dve.wait_ge(vs_ready, FROM + g + 1)
                                e = [at(ex, g2 * (2 * KINDS * GW) + (u * KINDS + i) * GW, GW) for i in range(KINDS)]
                                for i in range(BPG):
                                    cols = slice(i * T, (i + 1) * T)
                                    c.mark(nc.vector.tensor_tensor_scan(
                                        a_st[:, i * W1T + 1:(i + 1) * W1T], e[0][:, cols], new_v[u][:, cols],
                                        0.0, ALU.mult, ALU.add))
                                    c.mark(nc.vector.tensor_tensor_scan(
                                        b_st[:, i * W1T + 1:(i + 1) * W1T], e[0][:, cols], e[1][:, cols],
                                        0.0, ALU.mult, ALU.add))
                                c.wait()
                                n3, d3 = b3(num[:, :]), b3(den[:, :])
                                nc.vector.tensor_tensor(n3, b3(e[2]), b3(a_st[:, :], W1T)[:, :, 0:T], ALU.mult)
                                c.link(nc.vector.tensor_tensor(d3, b3(e[2]), b3(b_st[:, :], W1T)[:, :, 0:T], ALU.mult))
                                nc.vector.tensor_tensor(num[:, :], num[:, :], out_v[u][:, :], ALU.add).then_inc(vs_used, 1)
                                c.link(nc.vector.tensor_tensor(den[:, :], den[:, :], e[3], ALU.add))
                                nc.vector.tensor_tensor(num[:, :], num[:, :], at(r_all, g2 * (2 * GW) + u * GW, GW), ALU.mult)
                                c.link(nc.vector.reciprocal(den[:, :], den[:, :]))
                                dve.wait_ge(wo_ps, FROM + g)
                                nc.vector.tensor_tensor(wkv[:, :], num[:, :], den[:, :], ALU.mult).then_inc(wkv_ready, 1)
                                dve.wait_ge(wo_ps, FROM + g + 1)
                                h = at(h_tok, g2 * (2 * GW) + u * GW, GW)
                                nc.vector.tensor_tensor(h, ps[0][:, :], h, ALU.add).then_inc(wo_sb, 1)
                                assert c.n == steps, c.n

                    @block.scalar
                    def _(act):
                        with act.Fori(0, GROUPS) as g:
                            act.wait_ge(diffs, FROM + g + 1)
                            e = at(ex, g * (KINDS * GW), KINDS * GW)
                            nc.scalar.activation(e, e, ACT.Exp).then_inc(exped, 1)

                    @block.gpsimd
                    def _(pool):
                        with pool.Fori(0, GROUPS // 2) as g2:
                            for u in range(2):
                                pool.wait_ge(exped, FROM + g2 * 2 + u + 1)
                                pool.wait_ge(vs_used, FROM + g2 * 2)
                                v = at(v_all, g2 * (2 * GW) + u * GW, GW)
                                e = [at(ex, g2 * (2 * KINDS * GW) + (u * KINDS + i) * GW, GW) for i in range(KINDS)]
                                nc.gpsimd.tensor_tensor(new_v[u][:, :], e[1], v, ALU.mult)
                                nc.gpsimd.tensor_tensor(out_v[u][:, :], e[3], v, ALU.mult).then_inc(vs_ready, 1)

                    @block.tensor
                    def _(pe):
                        with pe.Fori(0, GROUPS) as g:
                            pe.wait_ge(wkv_ready, FROM + g + 1)
                            pe.wait_ge(wo_sb, FROM + g)
                            for t in range(TPG):
                                last = nc.tensor.matmul(ps[0][:, t * P:(t + 1) * P], wkv[:, t * P:(t + 1) * P],
                                                        mats["att_Wo"][:, :], start=True, stop=True)
                            last.then_inc(wo_ps, 1)

        with ExitStack() as s:
            def tb(name, cols, dt=F32, rows=P):
                return s.enter_context(nc.sbuf_tensor("f_" + name, [rows, cols], dt))
            xc = tb("xc", NB * W1T)
            load_norm_transpose("c4_", None, False, "ln2_g", "ln2_b", xc, False)
            sem = lambda n: env["semaphore"]("c5_" + n)
            mix_k, mix_r, tmp_k, tmp_r = (tb(n, GW) for n in ("mix_k", "mix_r", "tmp_k", "tmp_r"))
            relu = [tb(f"relu{i}", GW) for i in range(CH_RWKV)]
            kk = [tb(f"kk{i}", GW) for i in range(CH_RWKV)]
            sig, prod = tb("sig", GW), tb("prod", GW)
            ps_k = [s.enter_context(nc.psum_tensor(f"c5_k{i}", [P, GW], F32)) for i in range(CH_RWKV)]
            ps_r = s.enter_context(nc.psum_tensor("c5_r", [P, GW], F32))
            ps_v = [s.enter_context(nc.psum_tensor(f"c5_v{i}", [P, GW], F32)) for i in range(2)]
            own, mix_ready, mix_used, k_ps, k_sb, kk_ready, kk_used, r_ps, r_sb, v_ps, v_sb = map(
                sem, ("own", "mix_ready", "mix_used", "k_ps", "k_sb", "kk_ready", "kk_used", "r_ps", "r_sb", "v_ps", "v_sb"))
            with nc.Block() as block:
                @block.vector
                def _(dve):
                    with dve.Fori(0, GROUPS // 2) as g2:
                        for u in range(2):
                            g = g2 * 2 + u
                            c = Chain(dve, own, g * 3)
                            dve.wait_ge(mix_used, FROM + g)
                            mixed(c, xc, g, "cm_k", tmp_k, mix_k)
                            mixed(c, xc, g, "cm_r", tmp_r, mix_r).then_inc(mix_ready, 1)
                            dve.wait_ge(r_sb, FROM + g + 1)
                            dve.wait_ge(v_ps, FROM + g + 1)
                            c.link(nc.vector.tensor_tensor(prod[:, :], ps_v[u][:, :], sig[:, :], ALU.mult))
                            nc.vector.tensor_tensor(at(y_tok, g2 * (2 * GW) + u * GW, GW), prod[:, :],
                                                    at(h_tok, g2 * (2 * GW) + u * GW, GW), ALU.add).then_inc(v_sb, 1)

                @block.tensor
                def _(pe):
                    with pe.Fori(0, GROUPS // 2) as g2:
                        for u in range(2):
                            g = g2 * 2 + u
                            pe.wait_ge(mix_ready, FROM + g + 1)
                            for c in range(CH_RWKV):
                                pe.wait_ge(k_sb, FROM + g * CH_RWKV)
                                nc.tensor.matmul(ps_k[c][:, :], mats["ffn_Wk"][:, c * P:(c + 1) * P], mix_k[:, :],
                                                 start=True, stop=True).then_inc(k_ps, 1)
                            pe.wait_ge(r_sb, FROM + g)
                            for t in range(TPG):
                                last = nc.tensor.matmul(ps_r[:, t * P:(t + 1) * P], mix_r[:, t * P:(t + 1) * P],
                                                        mats["ffn_Wr"][:, :], start=True, stop=True)
                            last.then_inc(r_ps, 1)
                            pe.sem_inc(mix_used, 1)
                            pe.wait_ge(v_sb, FROM + g)
                            for c in range(CH_RWKV):
                                pe.wait_ge(kk_ready, FROM + g * CH_RWKV + c + 1)
                                for t in range(TPG):
                                    last = nc.tensor.matmul(ps_v[u][:, t * P:(t + 1) * P], kk[c][:, t * P:(t + 1) * P],
                                                            mats["ffn_Wv"][:, c * P:(c + 1) * P],
                                                            start=(c == 0 and t == 0), stop=(c == CH_RWKV - 1),
                                                            skip_group_check=True)
                            last.then_inc(v_ps, 1)

                @block.scalar
                def _(act):
                    with act.Fori(0, GROUPS) as g:
                        for c in range(CH_RWKV):
                            act.wait_ge(k_ps, FROM + g * CH_RWKV + c + 1)
                            act.wait_ge(kk_ready, FROM + g * CH_RWKV)
                            nc.scalar.activation(relu[c][:, :], ps_k[c][:, :], ACT.Relu).then_inc(k_sb, 1)
                        act.wait_ge(r_ps, FROM + g + 1)
                        act.wait_ge(v_sb, FROM + g)
                        nc.scalar.activation(sig[:, :], ps_r[:, :], ACT.Sigmoid).then_inc(r_sb, 1)

                @block.gpsimd
                def _(pool):
                    with pool.Fori(0, GROUPS) as g:
                        for c in range(CH_RWKV):
                            pool.wait_ge(k_sb, FROM + g * CH_RWKV + c + 1)
                            pool.wait_ge(v_ps, FROM + g)
                            nc.gpsimd.tensor_tensor(kk[c][:, :], relu[c][:, :], relu[c][:, :],
                                                    ALU.mult).then_inc(kk_ready, 1)


def laid_out(d):
    f = lambda n: np.asarray(d[n])
    c = np.ascontiguousarray
    w = {"x": f("L0_attn_hidden_states")}
    for n in ("Wq", "Wk", "Wv", "W1", "W2"):
        w[n] = f("L0_attn_" + n)
    for n in ("bq", "bk", "bv", "b1", "b2"):
        w[n] = f("L0_attn_" + n).reshape(-1, 1)
    w["router"] = f("L0_ffn_router_w").T
    w["router_bias"] = f("L0_ffn_router_bias").reshape(1, -1)
    w["gate0"] = f("L0_ffn_gate_w").transpose(2, 0, 1).reshape(P, -1)
    w["up0"] = f("L0_ffn_up_w").transpose(2, 0, 1).reshape(P, -1)
    w["down0"] = f("L0_ffn_down_w").transpose(2, 0, 1).reshape(P, -1)
    w["sgate0"] = f("L0_ffn_sgate_w").T
    w["sup0"] = f("L0_ffn_sup_w").T
    w["sdown0"] = f("L0_ffn_sdown_w").T.reshape(SH0, P, P).transpose(1, 0, 2).reshape(P, -1)
    for n in ("ln1_g", "ln1_b", "ln2_g", "ln2_b", "time_decay", "time_first", "time_mix_k", "time_mix_v",
              "time_mix_r", "cm_k", "cm_r"):
        w[n] = f("L1_attn_" + n).reshape(P, 1)
    for n in ("att_Wk", "att_Wv", "att_Wr", "att_Wo", "ffn_Wk", "ffn_Wr"):
        w[n] = f("L1_attn_" + n).T
    w["ffn_Wv"] = f("L1_attn_ffn_Wv").T.reshape(CH_RWKV, P, P).transpose(1, 0, 2).reshape(P, -1)
    w["gate_w1"] = f("L1_ffn_gate_w").T
    w["sw1"] = f("L1_ffn_shared_w1").T
    w["sw2"] = f("L1_ffn_shared_w2").T.reshape(CH1, P, P).transpose(1, 0, 2).reshape(P, -1)
    w["ew1"] = f("L1_ffn_experts_w1").transpose(2, 0, 1).reshape(P, -1)
    w["ew2"] = f("L1_ffn_experts_w2").reshape(E1, P, CH1, P).transpose(3, 0, 2, 1).reshape(P, -1)
    return {n: c(v) for n, v in w.items()}


def kernel(**inputs):
    import concourse.bacc as bacc
    from concourse.bass_utils import run_bass_kernel_spmd

    nc = bacc.Bacc("TRN2", target_bir_lowering=False, num_devices=1)
    arrays = laid_out(inputs)
    aps = {n: nc.dram_tensor("in_" + n, v.shape, mybir.dt.from_np(v.dtype), kind="ExternalInput").ap()
           for n, v in arrays.items()}
    out = nc.dram_tensor("result", (NB, T, P), F32, kind="ExternalOutput").ap()
    build(nc, aps, out)
    return run_bass_kernel_spmd(nc, [{"in_" + n: v for n, v in arrays.items()}], core_ids=[0]).results[0]["result"]
```

```python
import itertools
from contextlib import ExitStack

import numpy as np
import concourse.bass as bass
from concourse import mybir

F32 = mybir.dt.float32
F32R = mybir.dt.float32r
BF16 = mybir.dt.bfloat16
ALU = mybir.AluOpType
ACT = mybir.ActivationFunctionType
AX = mybir.AxisListType

P = 128
NB, T = 16, 256
TILES = NB * T // P
GROUPS = 8
TPG = TILES // GROUPS
GW = TPG * P
BPG = GW // T
TPB = T // P
N = TILES * P

HEADS, HD = 16, 8
HR = 32
LO, HI = 16, 16
VC = 2 * HD + 2
PARTS = 3
HQ = 4

E0, K0, SH0 = 32, 4, 4
E1, K1, CH1 = 8, 2, 4
CH_RWKV = 4
LN_EPS = 1e-5
STD_EPS = 1e-6
FROM = 1
NEVER = -1e38
OUTSIDE = -3e38


def at(tile, start, size=P):
    return tile[:, bass.ds(start, size)]


def pipelined(eng, n, step):
    assert n % 2 == 0
    step(0, 0)
    with eng.Fori(0, n // 2 - 1) as i2:
        step(i2 * 2 + 1, 1)
        step(i2 * 2 + 2, 0)
    step(n - 1, 1)
    step(n, 0)


def is_at(i, n):
    return isinstance(i, int) and i == n


def groups(eng, group):
    group(0, True)
    with eng.Fori(1, GROUPS) as g:
        group(g, False)


class Chain:

    def __init__(self, eng, sem, base=0):
        self.eng, self.sem, self.base, self.n = eng, sem, base, 0

    def mark(self, ins):
        self.n += 1
        ins.then_inc(self.sem, 1)

    def wait(self):
        self.eng.wait_ge(self.sem, FROM + self.base + self.n)

    def link(self, ins):
        self.mark(ins)
        self.wait()


def build(nc, a, out):
    top = ExitStack()
    with top:
        def keep(name, cols, dt=F32, rows=P):
            return top.enter_context(nc.sbuf_tensor(name, [rows, cols], dt))

        ready = []
        taken = []

        def ready_semaphores(n):
            engines = (nc.sync, nc.scalar, nc.vector, nc.gpsimd, nc.tensor)
            for i in range(n):
                ready.append(nc.alloc_semaphore(f"ready_{next(serial)}"))
                engines[i % len(engines)].sem_inc(ready[-1], FROM)
            nc.all_engine_barrier()

        def semaphore(name):
            taken.append(ready.pop())
            return taken[-1]

        def clear_semaphores(n):
            nc.clear_and_free_semaphores(taken + ready)
            taken.clear()
            ready.clear()
            nc.all_engine_barrier()
            ready_semaphores(n)

        serial = itertools.count()
        ready_semaphores(100)
        x_tok = keep("x_tok", N)
        y_tok = keep("y_tok", N)
        h_tok = keep("h_tok", N)
        ident = keep("ident", P)
        ones = keep("ones", P)
        eps_ln = keep("eps_ln", 1)
        eps_std = keep("eps_std", 1)
        stats = keep("stats", TILES * 6)
        mean = keep("mean", TILES)
        rstd = keep("rstd", TILES)
        spread = keep("spread", TILES)
        g_stats = keep("g_stats", TPG * 6)
        g_mean, g_rstd, g_spread = (keep(n, TPG) for n in ("g_mean", "g_rstd", "g_spread"))

        def row_stats(dve, src, done):
            with dve.Fori(0, GROUPS) as g:
                for t in range(TPG):
                    nc.vector.bn_stats(at(stats, g * (TPG * 6) + t * 6, 6),
                                       at(src, g * GW + t * P)).then_inc(done, 1)
            dve.wait_ge(done, FROM + TILES)

        def merge_stats(c, st, mean_, var_, tmp_, count):
            s = st.rearrange("p (t s) -> p t s", s=6)
            c.mark(nc.vector.tensor_tensor(mean_, s[:, :, 1], s[:, :, 4], ALU.add))
            c.link(nc.vector.tensor_tensor(tmp_, s[:, :, 1], s[:, :, 4], ALU.subtract))
            c.mark(nc.vector.tensor_scalar(mean_, mean_, 0.5, None, ALU.mult))
            c.link(nc.vector.tensor_tensor(tmp_, tmp_, tmp_, ALU.mult))
            c.mark(nc.vector.tensor_tensor(var_, s[:, :, 2], s[:, :, 5], ALU.add))
            c.link(nc.vector.tensor_scalar(tmp_, tmp_, count / 2, None, ALU.mult))
            c.link(nc.vector.tensor_tensor(var_, var_, tmp_, ALU.add))

        def norm_dve(dve, c, src, stats_done, var_ready, std_ready):
            if src is not None:
                row_stats(dve, src, stats_done)
            merge_stats(c, stats[:, :], mean[:, :], rstd[:, :], spread[:, :], P // 2)
            dve.sem_inc(var_ready, 1)
            dve.wait_ge(std_ready, FROM + 1)
            c.link(nc.vector.reciprocal(rstd[:, :], rstd[:, :]))

        def norm_act(act, var_ready, std_ready):
            act.wait_ge(var_ready, FROM + 1)
            nc.scalar.activation(rstd[:, :], rstd[:, :], ACT.Sqrt, bias=eps_ln[:, :],
                                 scale=1.0 / P).then_inc(std_ready, 1)

        def norm_rows(dve, src, dst, done, tiles=TPG):
            with dve.Fori(0, GROUPS) as g:
                for t in range(TPG):
                    last = nc.vector.tensor_scalar(
                        at(dst, g * GW + t * P), at(src, g * GW + t * P),
                        at(mean, g * TPG + t, 1), at(rstd, g * TPG + t, 1), ALU.subtract, ALU.mult)
                last.then_inc(done, 1)

        def residual_stats(dve, own, g, y, var_ready):
            c = Chain(dve, own, g * (TPG + 7))
            for t in range(TPG):
                c.mark(nc.vector.bn_stats(g_stats[:, t * 6:t * 6 + 6], y[:, t * P:(t + 1) * P]))
            c.wait()
            merge_stats(c, g_stats[:, :], g_mean[:, :], g_rstd[:, :], g_spread[:, :], P // 2)
            assert c.n == TPG + 7
            dve.sem_inc(var_ready, 1)

        def residual_std(act, g, var_ready, std_ready):
            act.wait_ge(var_ready, FROM + g + 1)
            nc.scalar.activation(g_rstd[:, :], g_rstd[:, :], ACT.Sqrt, bias=eps_ln[:, :],
                                 scale=1.0 / P).then_inc(std_ready, 1)

        def residual_norm(dve, g, y, std_ready, inverted, normed):
            dve.wait_ge(std_ready, FROM + g + 1)
            nc.vector.reciprocal(g_rstd[:, :], g_rstd[:, :]).then_inc(inverted, 1)
            dve.wait_ge(inverted, FROM + g + 1)
            for t in range(TPG):
                cols = slice(t * P, (t + 1) * P)
                last = nc.vector.tensor_scalar(y[:, cols], y[:, cols], g_mean[:, t:t + 1], g_rstd[:, t:t + 1],
                                               ALU.subtract, ALU.mult)
            last.then_inc(normed, 1)

        def residual_add(pool, g, normed, added):
            pool.wait_ge(normed, FROM + g + 1)
            nc.gpsimd.tensor_tensor(at(x_tok, g * GW, GW), at(x_tok, g * GW, GW),
                                    at(y_tok, g * GW, GW), ALU.add).then_inc(added, 1)

        def transposes(pe, src, banks, ready, done, evacuated):
            for g in range(GROUPS):
                pe.wait_ge(ready, FROM + g + 1)
                if g >= 2:
                    pe.wait_ge(evacuated, FROM + g - 1)
                for t in range(TPG):
                    o = (g * TPG + t) * P
                    last = nc.tensor.transpose(banks[g % 2][:, t * P:(t + 1) * P], src[:, o:o + P], ident[:, :])
                last.then_inc(done, 1)

        with ExitStack() as s:
            loaded, made = semaphore("x_loaded"), semaphore("constants_made")
            with nc.Block() as block:
                @block.sync
                def _(sp):
                    sp.dma_start(x_tok[:, :].rearrange("p (b u c) -> p b u c", u=TPB, c=P),
                                 a["x"].rearrange("b (u p) c -> p b u c", p=P)).then_inc(loaded, 16)
                    sp.wait_ge(loaded, FROM + 16)

                @block.vector
                def _(dve):
                    nc.vector.memset(ones[:, :], 1.0)
                    nc.vector.memset(eps_ln[:, :], LN_EPS)
                    nc.vector.memset(eps_std[:, :], STD_EPS)

                @block.gpsimd
                def _(pool):
                    nc.gpsimd.memset(ident[:, :], 0.0).then_inc(made, 1)
                    pool.wait_ge(made, FROM + 1)
                    nc.gpsimd.affine_select(out=ident[:, :], in_=ident[:, :], compare_op=ALU.not_equal,
                                            fill=1.0, base=0, pattern=[[-1, P]], channel_multiplier=1)

        attention0(nc, a, locals())
        add_normed(nc, locals(), stats_made=True)
        experts(nc, a, locals(), 0)
        clear_semaphores(90)
        rwkv(nc, a, locals())
        add_normed(nc, locals(), stats_made=True)
        clear_semaphores(50)
        experts(nc, a, locals(), 1)


def add_normed(nc, env, stats_made=False):
    x_tok, y_tok = env["x_tok"], env["y_tok"]
    with ExitStack() as s:
        sem = lambda n: env["semaphore"](n)
        stats_done, self_done, var_ready, std_ready, normed = map(
            sem, ("stats_done", "dve_done", "var_ready", "std_ready", "normed"))
        with nc.Block() as block:
            @block.vector
            def _(dve):
                c = Chain(dve, self_done)
                env["norm_dve"](dve, c, None if stats_made else y_tok, stats_done, var_ready, std_ready)
                env["norm_rows"](dve, y_tok, y_tok, normed)

            @block.scalar
            def _(act):
                env["norm_act"](act, var_ready, std_ready)

            @block.gpsimd
            def _(pool):
                with pool.Fori(0, GROUPS) as g:
                    pool.wait_ge(normed, FROM + g + 1)
                    nc.gpsimd.tensor_tensor(at(x_tok, g * GW, GW), at(x_tok, g * GW, GW),
                                            at(y_tok, g * GW, GW), ALU.add)


def attention0(nc, a, env):
    x_tok, y_tok, h_tok = env["x_tok"], env["y_tok"], env["h_tok"]
    ident, ones, eps_std = env["ident"], env["ones"], env["eps_std"]
    phase = ExitStack()
    with phase:
        def sb(name, cols, dt=F32, rows=P):
            return phase.enter_context(nc.sbuf_tensor(name, [rows, cols], dt))

        PR = 2 * HR
        proj = {"q": sb("proj_q", N, rows=PR), "k": sb("proj_k", N, rows=PR)}
        pstat = {w: sb(f"pstat_{w}", NB * 6, rows=PR) for w in "qk"}
        pmean = {w: sb(f"pmean_{w}", NB, rows=PR) for w in "qk"}
        pvar = {w: sb(f"pvar_{w}", NB, rows=PR) for w in "qk"}
        ptmp = sb("ptmp", NB, rows=PR)
        v_tok = sb("v_tok", N)

        with ExitStack() as s:
            def tb(name, cols, dt=F32, rows=P):
                return s.enter_context(nc.sbuf_tensor(name, [rows, cols], dt))
            sem = lambda n: env["semaphore"](n)
            ps = [s.enter_context(nc.psum_tensor(f"ps{i}", [P, GW], F32)) for i in range(8)]
            w = {n: tb(f"w_{n}", P) for n in ("Wv", "W1")}
            w_qk = tb("w_qk", 2 * P)
            b_qk = tb("b_qk", 2 * P)
            w2 = tb("w2", PR)
            b = {n: tb(f"b_{n}", 1) for n in ("bv", "b1")}
            b2 = tb("b2", 1, rows=PR)
            h_fm = tb("h_fm", N)
            qk_tok = tb("qk_tok", LO * 2 * P)
            rows_fm = {"q": h_tok, "k": y_tok}
            v_fm, v_cent = tb("v_fm", GW), tb("v_cent", GW)
            gelu = {x: tb(f"gelu_{x}", GW) for x in "qk"}
            part_weight = tb("part_weight", 1)
            vstat, vmean = tb("vstat", BPG * 6), tb("vmean", BPG)
            weights, cleared = sem("weights"), sem("w2_cleared")
            WLOADS = len(w) + len(b) + 4 + 4
            stats_done, self_done, var_ready, std_ready = map(
                sem, ("stats_done", "dve_done", "var_ready", "std_ready"))
            rows_ready, fm_ps, fm_sb = sem("rows_ready"), sem("fm_ps"), sem("fm_sb")
            v_ps, v_sb = sem("v_ps"), sem("v_sb")
            qk_ps, qk_sb, turned_ps, turned_sb = map(sem, ("qk_ps", "qk_sb", "turned_ps", "turned_sb"))
            up_ps = {x: sem(f"up_{x}_ps") for x in "qk"}
            up_sb = {x: sem(f"up_{x}_sb") for x in "qk"}
            pr_ps = {x: sem(f"pr_{x}_ps") for x in "qk"}
            pr_sb = {x: sem(f"pr_{x}_sb") for x in "qk"}
            pstats_done = sem("pstats_done")
            v_self, centred, vt_ps, vt_sb = sem("v_self"), sem("centred"), sem("vt_ps"), sem("vt_sb")
            NQ = LO // 2
            NTURN = 2 * HEADS // TPG
            up = {"q": ps[3], "k": ps[4]}
            down = {"q": ps[5], "k": ps[6]}
            with nc.Block() as block:
                @block.sync
                def _(sp):
                    for n in w:
                        sp.dma_start(w[n][:, :], a[n]).then_inc(weights, 16)
                    for n in b:
                        sp.dma_start(b[n][:, :], a[n]).then_inc(weights, 16)
                    for i, n in enumerate("qk"):
                        sp.dma_start(w_qk[:, i * P:(i + 1) * P], a["W" + n]).then_inc(weights, 16)
                        sp.dma_start(b_qk[:, i * P:(i + 1) * P],
                                     a["b" + n].rearrange("c o -> o c").partition_broadcast(P)).then_inc(weights, 16)
                    sp.wait_ge(cleared, FROM + 4)
                    for r in range(2):
                        sp.dma_start(w2[:, r * HR:r * HR + HEADS], a["W2"]).then_inc(weights, 16)
                        sp.dma_start(b2[r * HR:r * HR + HEADS, :], a["b2"]).then_inc(weights, 16)

                @block.gpsimd
                def _(pool):
                    nc.gpsimd.memset(w2[:, :], 0.0).then_inc(cleared, 1)
                    nc.gpsimd.memset(b2[:, :], 0.0).then_inc(cleared, 1)
                    pool.wait_ge(cleared, FROM + 2)
                    nc.gpsimd.memset(part_weight[0:P // 2, :], 1.0).then_inc(cleared, 1)
                    nc.gpsimd.memset(part_weight[P // 2:P, :], 0.5).then_inc(cleared, 1)

                @block.tensor
                def _(pe):
                    env["transposes"](pe, h_tok, ps[6:8], rows_ready, fm_ps, fm_sb)
                    pe.wait_ge(weights, FROM + WLOADS * 16)
                    pe.wait_ge(fm_sb, FROM + GROUPS)
                    hf = h_fm[:, :].rearrange("p (b t l) -> p l b t", t=HI, l=LO)
                    for half in range(2):
                        if half:
                            pe.wait_ge(turned_ps, FROM + NTURN)
                        for i in range(NQ):
                            n = half * NQ + i
                            if n >= 2:
                                pe.wait_ge(qk_sb, FROM + n - 1)
                            for l in range(2):
                                last = nc.tensor.matmul(ps[n % 2][:, l * 2 * P:(l + 1) * 2 * P],
                                                        hf[:, 2 * i + l, half * NB // 2:(half + 1) * NB // 2, :],
                                                        w_qk[:, :], start=True, stop=True)
                            last.then_inc(qk_ps, 1)
                        pe.wait_ge(qk_sb, FROM + (half + 1) * NQ)
                        for i in range(NTURN):
                            n = half * NTURN + i
                            if n >= 2:
                                pe.wait_ge(turned_sb, FROM + n - 1)
                            for t in range(TPG):
                                o = (i * TPG + t) * P
                                last = nc.tensor.transpose(ps[2 + n % 2][:, t * P:(t + 1) * P],
                                                           qk_tok[:, o:o + P], ident[:, :])
                            last.then_inc(turned_ps, 1)
                    pe.wait_ge(turned_sb, FROM + 2 * NTURN)

                    def step(g, u):
                        if not is_at(g, GROUPS):
                            pe.wait_ge(v_sb, FROM + g)
                            nc.tensor.matmul(ps[2][:, :], w["Wv"][:, :], at(h_fm, g * GW, GW),
                                             start=True, stop=True).then_inc(v_ps, 1)
                            for x in "qk":
                                pe.wait_ge(up_sb[x], FROM + g)
                                nc.tensor.matmul(up[x][:, :], w["W1"][:, :], at(rows_fm[x], g * GW, GW),
                                                 start=True, stop=True).then_inc(up_ps[x], 1)
                        if not is_at(g, 0):
                            for x in "qk":
                                pe.wait_ge(up_sb[x], FROM + g)
                                pe.wait_ge(pr_sb[x], FROM + g - 1)
                                nc.tensor.matmul(down[x][0:PR, :], w2[:, :], gelu[x][:, :],
                                                 start=True, stop=True).then_inc(pr_ps[x], 1)
                        if not is_at(g, GROUPS):
                            pe.wait_ge(centred, FROM + g + 1)
                            pe.wait_ge(vt_sb, FROM + g)
                            for t in range(TPG):
                                last = nc.tensor.transpose(ps[7][:, t * P:(t + 1) * P],
                                                           v_cent[:, t * P:(t + 1) * P], ident[:, :])
                            last.then_inc(vt_ps, 1)
                    pipelined(pe, GROUPS, step)

                @block.scalar
                def _(act):
                    env["norm_act"](act, var_ready, std_ready)
                    with act.Fori(0, GROUPS // 2) as g2:
                        for u in range(2):
                            act.wait_ge(fm_ps, FROM + g2 * 2 + u + 1)
                            nc.scalar.activation(at(h_fm, g2 * (2 * GW) + u * GW, GW), ps[6 + u][:, :],
                                                 ACT.Copy).then_inc(fm_sb, 1)
                    for n in range(2 * NTURN):
                        half, x, hq = n // NTURN, n % NTURN // (NTURN // 2), n % (NTURN // 2)
                        act.wait_ge(turned_ps, FROM + n + 1)
                        dst = rows_fm["qk"[x]][:, :].rearrange("p (b h t) -> p h b t", h=HEADS, t=HI)
                        nc.scalar.activation(
                            dst[:, hq * TPG:(hq + 1) * TPG, half * NB // 2:(half + 1) * NB // 2, :],
                            ps[2 + n % 2][:, :].rearrange("p (h b t) -> p h b t", h=TPG, t=HI),
                            ACT.Copy).then_inc(turned_sb, 1)
                    act.wait_ge(weights, FROM + WLOADS * 16)
                    with act.Fori(0, GROUPS) as g:
                        for x in "qk":
                            act.wait_ge(up_ps[x], FROM + g + 1)
                            act.wait_ge(pr_ps[x], FROM + g)
                            nc.scalar.activation(gelu[x][:, :], up[x][:, :], ACT.Gelu,
                                                 bias=b["b1"][:, :]).then_inc(up_sb[x], 1)

                @block.vector
                def _(dve):
                    c = Chain(dve, self_done)
                    env["norm_dve"](dve, c, x_tok, stats_done, var_ready, std_ready)
                    env["norm_rows"](dve, x_tok, h_tok, rows_ready)
                    dve.wait_ge(weights, FROM + WLOADS * 16)
                    for n in range(2 * NQ):
                        half, i = n // NQ, n % NQ
                        dve.wait_ge(qk_ps, FROM + n + 1)
                        if half:
                            dve.wait_ge(turned_ps, FROM + NTURN)
                        nc.vector.tensor_tensor(
                            qk_tok[:, :].rearrange("p (h l d) -> p l h d", l=LO, d=HD)[:, 2 * i:2 * i + 2],
                            ps[n % 2][:, :].rearrange("p (l h d) -> p l h d", l=2, d=HD),
                            b_qk[:, :].rearrange("p (h d) -> p h d", d=HD).unsqueeze(1).broadcast_to(
                                [P, 2, 2 * HEADS, HD]), ALU.add).then_inc(qk_sb, 1)
                    steps = 2 + 2 * BPG

                    def centre(g):
                        c = Chain(dve, v_self, g * steps)
                        dve.wait_ge(v_ps, FROM + g + 1)
                        nc.vector.tensor_scalar(v_fm[:, :], ps[2][:, :], b["bv"][:, :], None,
                                                ALU.add).then_inc(v_sb, 1)
                        dve.wait_ge(v_sb, FROM + g + 1)
                        for i in range(BPG):
                            c.mark(nc.vector.bn_stats(vstat[:, i * 6:i * 6 + 6], v_fm[:, i * T:(i + 1) * T]))
                        c.wait()
                        sv = vstat[:, :].rearrange("p (t s) -> p t s", s=6)
                        c.link(nc.vector.tensor_tensor(vmean[:, :], sv[:, :, 1], sv[:, :, 4], ALU.add))
                        c.link(nc.vector.tensor_scalar(vmean[:, :], vmean[:, :], 0.5, None, ALU.mult))
                        dve.wait_ge(vt_ps, FROM + g)
                        for i in range(BPG):
                            last = nc.vector.tensor_scalar(v_cent[:, i * T:(i + 1) * T], v_fm[:, i * T:(i + 1) * T],
                                                           vmean[:, i:i + 1], part_weight[:, :],
                                                           ALU.subtract, ALU.mult)
                            c.mark(last)
                        c.wait()
                        dve.sem_inc(centred, 1)
                        assert c.n == steps

                    def projections(g):
                        for x in "qk":
                            dve.wait_ge(pr_ps[x], FROM + g + 1)
                            nc.vector.tensor_scalar(at(proj[x], g * GW, GW), down[x][0:PR, :], b2[:, :], None,
                                                    ALU.add).then_inc(pr_sb[x], 1)
                        for x in "qk":
                            dve.wait_ge(pr_sb[x], FROM + g + 1)
                            for i in range(BPG):
                                nc.vector.bn_stats(at(pstat[x], g * (BPG * 6) + i * 6, 6),
                                                   at(proj[x], g * GW + i * T, T)).then_inc(pstats_done, 1)

                    def step(g, u):
                        if not is_at(g, GROUPS):
                            centre(g)
                        if not is_at(g, 0):
                            projections(g - 1)
                        if not is_at(g, GROUPS):
                            dve.wait_ge(vt_ps, FROM + g + 1)
                            nc.vector.tensor_copy(at(v_tok, g * GW, GW), ps[7][:, :]).then_inc(vt_sb, 1)
                    pipelined(dve, GROUPS, step)
                    dve.wait_ge(pstats_done, FROM + GROUPS * 2 * BPG)

        with ExitStack() as s:
            def tb(name, cols, dt=F32, rows=P):
                return s.enter_context(nc.sbuf_tensor(name, [rows, cols], dt))
            sem = lambda n: env["semaphore"](n)
            psq = [s.enter_context(nc.psum_tensor(f"ps_q{i}", [P, HQ * T], F32)) for i in range(2)]
            pso = [s.enter_context(nc.psum_tensor(f"ps_o{i}", [P, GW], F32)) for i in range(2 * TPB)]
            q_parts = tb("q_parts", N, F32R)
            pick = tb("pick", HEADS * P, F32R)
            q_tok, k_tok = tb("q_tok", TILES * HEADS), tb("k_tok", TILES * HEADS)
            k_sum = tb("k_sum", NB * HEADS)
            qn, kn = tb("qn", T), tb("kn", T)
            hi_r = tb("hi_r", T, F32R, rows=PR)
            cols = tb("cols", HEADS * VC)
            rest = tb("rest", HEADS * VC)
            vals = [tb(f"vals{i}", TPB * HEADS * PARTS * VC, BF16) for i in range(2)]
            QS = HEADS // HQ
            mask = [[[tb(f"mask{u}{q}{j}", HQ * T, BF16) for j in range(TPB)] for q in range(QS)] for u in range(2)]
            ones_bf = tb("ones_bf", P, BF16)
            head_weight = tb("head_weight", HEADS)
            k_neg = [tb(f"k_neg{u}", TPB * HEADS) for u in range(2)]
            sums = tb("sums", TPB * HEADS * VC)
            num = tb("num", T)
            n1, n2 = tb("n1", TPB * HEADS), tb("n2", TPB * HEADS)
            self_done, var_ready, std_ready = map(sem, ("dve_done", "var_ready", "std_ready"))
            prep, qk_rows, qk_ps, qk_sb = sem("prep"), sem("qk_rows"), sem("qk_ps"), sem("qk_sb")
            ksum_ps, ksum_sb = sem("ksum_ps"), sem("ksum_sb")
            pick_made, rows_cleared = sem("pick_made"), sem("rows_cleared")
            cols_self, cols_ready, hi_ready, mid_ready, rest_ready = map(
                sem, ("cols_self", "cols_ready", "hi_ready", "mid_ready", "rest_ready"))
            vals_ready = sem("vals_ready")
            q_ps_dve, q_ps_act, masks_dve, masks_act, neg_ready, masked, sums_out = map(
                sem, ("q_ps_dve", "q_ps_act", "masks_dve", "masks_act", "neg_ready", "masked", "sums_out"))
            batch_self, stats_done = sem("batch_self"), sem("stats_done")
            stats = env["stats"]
            HALF = HEADS // 2
            HV = PARTS * VC
            with nc.Block() as block:
                @block.vector
                def _(dve):
                    c = Chain(dve, self_done)
                    for x in "qk":
                        env["merge_stats"](c, pstat[x][:, :], pmean[x][:, :], pvar[x][:, :], ptmp[:, :], T // 2)
                    c.link(nc.vector.tensor_tensor(pvar["q"][:, :], pvar["q"][:, :], pvar["k"][:, :], ALU.add))
                    dve.sem_inc(var_ready, 1)
                    dve.wait_ge(std_ready, FROM + 1)
                    c.link(nc.vector.reciprocal(pvar["q"][:, :], pvar["q"][:, :]))
                    rs = pvar["q"]
                    steps = 4
                    with dve.Fori(0, NB) as b_:
                        c = Chain(dve, prep, b_ * steps)
                        dve.wait_ge(qk_ps, FROM + b_)
                        c.mark(nc.vector.tensor_scalar(qn[0:PR, :], at(proj["q"], b_ * T, T), at(pmean["q"], b_, 1),
                                                       at(rs, b_, 1), ALU.subtract, ALU.mult))
                        c.link(nc.vector.tensor_scalar(kn[0:PR, :], at(proj["k"], b_ * T, T), at(pmean["k"], b_, 1),
                                                       at(rs, b_, 1), ALU.subtract, ALU.mult))
                        dve.sem_inc(qk_rows, 1)
                        nc.vector.tensor_copy(q_parts[0:HR, bass.ds(b_ * T, T)], qn[0:HR, :])
                        c.link(nc.vector.tensor_copy(hi_r[HR:PR, :], qn[HR:PR, :]))
                        c.link(nc.vector.tensor_tensor(q_parts[HR:PR, bass.ds(b_ * T, T)], qn[HR:PR, :],
                                                       hi_r[HR:PR, :].bitcast(F32), ALU.subtract))
                        assert c.n == steps
                    steps = 11

                    def masks(b_, parity):
                        for quad in range(QS // 2):
                            dve.wait_ge(q_ps_dve, FROM + b_ * (QS // 2) + quad + 1)
                            for j in range(TPB):
                                keys = k_tok[:, bass.ds(b_ * (TPB * HEADS) + j * HEADS + quad * HQ, HQ)]
                                last = nc.vector.tensor_tensor(
                                    mask[parity][quad][j][:, :].rearrange("p (h t) -> p h t", t=T),
                                    psq[0][:, :].rearrange("p (h t) -> p h t", t=T),
                                    keys.unsqueeze(2).broadcast_to([P, HQ, T]), ALU.is_ge)
                            last.then_inc(masks_dve, 1)

                    def results(b_):
                        c = Chain(dve, batch_self, b_ * steps)
                        dve.wait_ge(masked, FROM + (b_ + 1) * QS)
                        for u in range(TPB):
                            for half in range(2):
                                o = (u * HEADS + half * HALF) * VC
                                last = nc.vector.tensor_reduce(
                                    sums[:, o:o + HALF * VC].rearrange("p (h r) -> p h r", r=VC),
                                    pso[u * 2 + half][:, 0:HALF * HV].rearrange("p (h s r) -> p h r s", s=PARTS, r=VC),
                                    axis=AX.X, op=ALU.add)
                        last.then_inc(sums_out, 1)
                        dve.wait_ge(sums_out, FROM + b_ + 1)
                        S = sums[:, :].rearrange("p (h r) -> p h r", r=VC)
                        q = at(q_tok, b_ * (TPB * HEADS), TPB * HEADS)
                        q_b = q.unsqueeze(2).broadcast_to([P, TPB * HEADS, HD])
                        num3 = num[:, :].rearrange("p (h r) -> p h r", r=HD)
                        c.mark(nc.vector.tensor_tensor(n1[:, :], S[:, :, 2 * HD], q, ALU.mult))
                        c.mark(nc.vector.tensor_scalar(n2[:, :], q, float(T), None, ALU.mult))
                        c.link(nc.vector.tensor_tensor(num3, S[:, :, 0:HD], q_b, ALU.mult))
                        c.mark(nc.vector.tensor_tensor(n1[:, :], n1[:, :], S[:, :, 2 * HD + 1], ALU.subtract))
                        ks = at(k_sum, b_ * HEADS, HEADS).unsqueeze(1).broadcast_to([P, TPB, HEADS])
                        c.mark(nc.vector.tensor_tensor(n2[:, :].rearrange("p (u h) -> p u h", h=HEADS),
                                                       n2[:, :].rearrange("p (u h) -> p u h", h=HEADS), ks, ALU.subtract))
                        c.link(nc.vector.tensor_tensor(num3, num3, S[:, :, HD:2 * HD], ALU.subtract))
                        c.link(nc.vector.scalar_tensor_tensor(n1[:, :], n1[:, :], 2.0, n2[:, :], ALU.mult, ALU.subtract))
                        c.link(nc.vector.tensor_scalar(n1[:, :], n1[:, :], 1e-4, None, ALU.max))
                        c.link(nc.vector.reciprocal(n1[:, :], n1[:, :]))
                        c.link(nc.vector.tensor_scalar(n1[:, :], n1[:, :], 2.0, None, ALU.mult))
                        c.link(nc.vector.tensor_tensor(at(y_tok, b_ * T, T).rearrange("p (h r) -> p h r", r=HD), num3,
                                                       n1[:, :].unsqueeze(2).broadcast_to([P, TPB * HEADS, HD]), ALU.mult))
                        assert c.n == steps, c.n
                        for t in range(TPB):
                            nc.vector.bn_stats(at(stats, b_ * (TPB * 6) + t * 6, 6),
                                               at(y_tok, b_ * T + t * P)).then_inc(stats_done, 1)

                    def step(b_, parity):
                        if not is_at(b_, NB):
                            masks(b_, parity)
                        if not is_at(b_, 0):
                            results(b_ - 1)
                    pipelined(dve, NB, step)
                    dve.wait_ge(stats_done, FROM + TILES)

                @block.scalar
                def _(act):
                    act.wait_ge(var_ready, FROM + 1)
                    nc.scalar.activation(pvar["q"][:, :], pvar["q"][:, :], ACT.Sqrt, bias=eps_std[0:PR, :],
                                         scale=0.5 / T).then_inc(std_ready, 1)
                    with act.Fori(0, NB) as b_:
                        act.wait_ge(qk_ps, FROM + b_ + 1)
                        for x, dst in enumerate((q_tok, k_tok)):
                            last = nc.scalar.activation(
                                at(dst, b_ * (TPB * HEADS), TPB * HEADS).rearrange("p (u h) -> p u h", h=HEADS),
                                pso[0][:, x * TPB * P:(x + 1) * TPB * P].rearrange(
                                    "p (u h) -> p u h", h=P)[:, :, 0:HEADS], ACT.Copy)
                        last.then_inc(qk_sb, 1)
                        act.wait_ge(ksum_ps, FROM + b_ + 1)
                        nc.scalar.activation(at(k_sum, b_ * HEADS, HEADS), pso[1][:, 0:HEADS],
                                             ACT.Copy).then_inc(ksum_sb, 1)
                    with act.Fori(0, NB // 2) as b2_:
                        for u in range(2):
                            act.wait_ge(q_ps_act, FROM + b2_ * QS + u * (QS // 2) + 1)
                            nc.scalar.activation(k_neg[u][:, :], at(k_tok, b2_ * (2 * TPB * HEADS) + u * TPB * HEADS,
                                                                    TPB * HEADS),
                                                 ACT.Copy, scale=-1.0).then_inc(neg_ready, 1)
                            for j in range(TPB):
                                tile = b2_ * (2 * TPB) + u * TPB + j
                                part = vals[u][:, j * HEADS * HV:(j + 1) * HEADS * HV].rearrange(
                                    "p (h s r) -> p h s r", s=PARTS, r=VC)

                                def signs(keys):
                                    for h in range(HQ):
                                        head = (QS // 2 + j) * HQ + h
                                        last = nc.scalar.activation(
                                            mask[u][QS // 2 + j][keys][:, h * T:(h + 1) * T],
                                            psq[1][:, h * T:(h + 1) * T], ACT.Sign,
                                            bias=k_neg[u][:, keys * HEADS + head:keys * HEADS + head + 1])
                                    return last

                                act.wait_ge(cols_ready, FROM + tile + 1)
                                nc.scalar.activation(part[:, :, 0, :], cols[:, :].rearrange(
                                    "p (h r) -> p h r", r=VC), ACT.Copy).then_inc(hi_ready, 1)
                                if j == 0:
                                    act.wait_ge(neg_ready, FROM + b2_ * 2 + u + 1)
                                else:
                                    act.wait_ge(q_ps_act, FROM + b2_ * QS + u * (QS // 2) + 2)
                                signs(0)
                                act.wait_ge(rest_ready, FROM + tile + 1)
                                nc.scalar.activation(part[:, :, 1, :], rest[:, :].rearrange(
                                    "p (h r) -> p h r", r=VC), ACT.Copy).then_inc(mid_ready, 1)
                                signs(1).then_inc(masks_act, 1)

                @block.gpsimd
                def _(pool):
                    nc.gpsimd.memset(qn[PR:P, :], 0.0).then_inc(rows_cleared, 1)
                    nc.gpsimd.memset(kn[PR:P, :], 0.0).then_inc(rows_cleared, 1)
                    nc.gpsimd.memset(q_parts[PR:P, :].bitcast(F32), 0.0).then_inc(rows_cleared, 1)
                    pool.wait_ge(rows_cleared, FROM + 3)
                    nc.gpsimd.memset(pick[:, :].bitcast(F32), 0.0).then_inc(pick_made, 1)
                    pool.wait_ge(pick_made, FROM + 1)
                    for r in range(2):
                        dst = pick[r * HR:r * HR + HR, :].rearrange("p (h t) -> p h t", t=P)
                        nc.gpsimd.affine_select(out=dst, in_=pick[r * HR:r * HR + HR, :].bitcast(F32).rearrange(
                            "p (h t) -> p h t", t=P), compare_op=ALU.not_equal, fill=1.0, base=0,
                            pattern=[[-1, HEADS], [0, P]], channel_multiplier=1).then_inc(pick_made, 1)
                    pool.wait_ge(pick_made, FROM + 3)
                    nc.gpsimd.memset(ones_bf[:, :], 1.0).then_inc(pick_made, 1)
                    nc.gpsimd.memset(head_weight[:, 0:HALF], 1.0).then_inc(pick_made, 1)
                    nc.gpsimd.memset(head_weight[:, HALF:HEADS], 0.5).then_inc(pick_made, 1)
                    pool.wait_ge(pick_made, FROM + 6)
                    c3 = cols[:, :].rearrange("p (h r) -> p h r", r=VC)
                    nc.gpsimd.tensor_copy(c3[:, :, 2 * HD], head_weight[:, :])
                    r3 = rest[:, :].rearrange("p (h r) -> p h r", r=VC)
                    with pool.Fori(0, NB // 2) as b2_:
                        for u in range(2):
                            for j in range(TPB):
                                tile = b2_ * (2 * TPB) + u * TPB + j
                                part = vals[u][:, j * HEADS * HV:(j + 1) * HEADS * HV].rearrange(
                                    "p (h s r) -> p h s r", s=PARTS, r=VC)
                                pool.wait_ge(qk_sb, FROM + b2_ * 2 + u + 1)
                                pool.wait_ge(hi_ready, FROM + tile)
                                v3 = at(v_tok, tile * P, P).rearrange("p (h r) -> p h r", r=HD)
                                k2 = at(k_tok, tile * HEADS, HEADS)
                                nc.gpsimd.tensor_copy(c3[:, :, 0:HD], v3)
                                nc.gpsimd.tensor_tensor(c3[:, :, HD:2 * HD], v3,
                                                        k2.unsqueeze(2).broadcast_to([P, HEADS, HD]), ALU.mult)
                                nc.gpsimd.tensor_tensor(c3[:, :, 2 * HD + 1], k2, head_weight[:, :],
                                                        ALU.mult).then_inc(cols_ready, 1)
                                pool.wait_ge(hi_ready, FROM + tile + 1)
                                pool.wait_ge(mid_ready, FROM + tile)
                                nc.gpsimd.tensor_tensor(r3, c3, part[:, :, 0, :], ALU.subtract).then_inc(rest_ready, 1)
                                pool.wait_ge(mid_ready, FROM + tile + 1)
                                ins = nc.gpsimd.tensor_tensor(part[:, :, 2, :], r3, part[:, :, 1, :], ALU.subtract)
                            ins.then_inc(vals_ready, 1)

                @block.tensor
                def _(pe):
                    pe.wait_ge(rows_cleared, FROM + 3)
                    with pe.Fori(0, NB) as b_:
                        pe.wait_ge(qk_rows, FROM + b_ + 1)
                        pe.wait_ge(qk_sb, FROM + b_)
                        for x, src in enumerate((qn, kn)):
                            for t in range(TPB):
                                o = (x * TPB + t) * P
                                last = nc.tensor.transpose(pso[0][:, o:o + P], src[:, t * P:(t + 1) * P],
                                                           ident[:, :])
                        last.then_inc(qk_ps, 1)
                        pe.wait_ge(qk_sb, FROM + b_ + 1)
                        pe.wait_ge(ksum_sb, FROM + b_)
                        for t in range(TPB):
                            last = nc.tensor.matmul(pso[1][:, 0:HEADS], ones[:, :],
                                                    at(k_tok, b_ * (TPB * HEADS) + t * HEADS, HEADS),
                                                    start=(t == 0), stop=(t == TPB - 1))
                        last.then_inc(ksum_ps, 1)
                    pe.wait_ge(ksum_sb, FROM + NB)
                    pe.wait_ge(pick_made, FROM + 6)
                    pe.wait_ge(prep, FROM + NB * 4)

                    def spread_q(b_, quad):
                        on_dve = quad < QS // 2
                        done, read = (q_ps_dve, masks_dve) if on_dve else (q_ps_act, masks_act)
                        nth = quad % (QS // 2)
                        pe.wait_ge(read, FROM + b_ * (QS // 2) + nth)
                        for h in range(HQ):
                            last = nc.tensor.matmul(psq[0 if on_dve else 1][:, h * T:(h + 1) * T],
                                                    pick[:, (quad * HQ + h) * P:(quad * HQ + h + 1) * P],
                                                    q_parts[:, bass.ds(b_ * T, T)], start=True, stop=True)
                        last.then_inc(done, 1)

                    def mask_values(b_, parity, quad):
                        signs = quad >= QS // 2
                        if quad == 0:
                            pe.wait_ge(masks_dve, FROM + (b_ + 1) * (QS // 2))
                            pe.wait_ge(vals_ready, FROM + b_ + 1)
                            pe.wait_ge(sums_out, FROM + b_)
                        if quad == QS // 2:
                            pe.wait_ge(masks_act, FROM + (b_ + 1) * (QS // 2))
                            for ic in range(TPB):
                                for j in range(TPB):
                                    vo = (j * HEADS + HALF) * HV
                                    nc.tensor.matmul(pso[ic * 2 + 1][:, 0:HALF * HV], ones_bf[:, :],
                                                     vals[parity][:, vo:vo + HALF * HV], start=(j == 0), stop=False,
                                                     skip_group_check=True)
                        for h in range(HQ):
                            head = quad * HQ + h
                            o = (head % HALF) * HV
                            for ic in range(TPB):
                                for j in range(TPB):
                                    vo = (j * HEADS + head) * HV
                                    last = nc.tensor.matmul(
                                        pso[ic * 2 + head // HALF][:, o:o + HV],
                                        mask[parity][quad][j][:, h * T + ic * P:h * T + ic * P + P],
                                        vals[parity][:, vo:vo + HV], start=(j == 0 and not signs),
                                        stop=(j == TPB - 1), skip_group_check=True)
                        last.then_inc(masked, 1)

                    def step(b_, parity):
                        now, before = not is_at(b_, NB), not is_at(b_, 0)
                        if now:
                            spread_q(b_, 0)
                        if before:
                            mask_values(b_ - 1, 1 - parity, 0)
                            mask_values(b_ - 1, 1 - parity, 1)
                        if now:
                            spread_q(b_, 2)
                        if before:
                            mask_values(b_ - 1, 1 - parity, 2)
                        if now:
                            spread_q(b_, 1)
                        if before:
                            mask_values(b_ - 1, 1 - parity, 3)
                        if now:
                            spread_q(b_, 3)
                    pipelined(pe, NB, step)


def experts(nc, a, env, layer):
    x_tok, y_tok, h_tok, ident = env["x_tok"], env["y_tok"], env["h_tok"], env["ident"]
    gated = layer == 0
    E, K = ((E0, K0), (E1, K1))[layer]
    CH = 1 if gated else CH1
    pre = f"e{layer}_"
    LW = E + 8
    outside = -1.0 if gated else OUTSIDE
    if gated:
        UPS = [("gate0", E * P), ("up0", E * P), ("sgate0", SH0 * P), ("sup0", SH0 * P)]
        DOWNS = [("down0", E * P), ("sdown0", SH0 * P)]
    else:
        UPS = [("ew1", E * CH * P), ("sw1", CH * P)]
        DOWNS = [("ew2", E * CH * P), ("sw2", CH * P)]
    phase = ExitStack()
    with phase:
        def sb(name, cols, dt=F32, rows=P):
            return phase.enter_context(nc.sbuf_tensor(pre + name, [rows, cols], dt))

        h_hi, h_lo = sb("h_hi", N, F32R), sb("h_lo", N, F32R)
        SPLIT = UPS if gated else UPS + DOWNS
        w_hi = {n: sb(n + "_hi", c, F32R) for n, c in SPLIT}
        w_lo = {n: sb(n + "_lo", c, F32R) for n, c in SPLIT}
        w_down = {n: sb(n, c) for n, c in DOWNS} if gated else {}
        if not gated:
            gates_fm = h_tok
            selector = sb("selector", E * P, F32R)
        gates = sb("gates", TILES * E)

        with ExitStack() as s:
            def tb(name, cols, dt=F32, rows=P):
                return s.enter_context(nc.sbuf_tensor(pre + name, [rows, cols], dt))
            sem = lambda n: env["semaphore"](pre + n)
            ps = [s.enter_context(nc.psum_tensor(f"{pre}ps{i}", [P, GW], F32)) for i in range(4)]
            router = tb("router", E)
            bias = tb("bias", E)
            h_fm = [tb(f"h_fm{i}", GW) for i in range(2)]
            logits = tb("logits", TILES * LW)
            left = tb("left", TILES * LW)
            best, chosen = tb("best", TILES * 8), tb("chosen", TILES * 8)
            total = tb("total", TILES)
            SC = 512
            stage = [tb(f"stage{i}", SC) for i in range(2)]
            pieces = [(n, o) for n, c in SPLIT for o in range(0, c, SC)]
            staged = [sem("staged0"), sem("staged1")]
            small, downs = sem("small"), sem("downs")
            stats_done, self_done, var_ready, std_ready = map(
                sem, ("stats_done", "dve_done", "var_ready", "std_ready"))
            rows_ready, fm_ps, fm_sb, split, logit_ps, logit_sb = map(
                sem, ("rows_ready", "fm_ps", "fm_sb", "split", "logit_ps", "logit_sb"))
            hi_made, lo_made = sem("hi_made"), sem("lo_made")
            shifted, exped = sem("shifted"), sem("exped")
            if not gated:
                gates_hi, gates_2 = tb("gates_hi", TILES * E, F32R), tb("gates_2", TILES * 2 * E)
                parts_ready, gates_ps, gates_sb = sem("parts_ready"), sem("gates_ps"), sem("gates_sb")
            L = logits[:, :].rearrange("p (t e) -> p t e", e=LW)
            R = left[:, :].rearrange("p (t e) -> p t e", e=LW)
            B = best[:, :].rearrange("p (t e) -> p t e", e=8)
            C = chosen[:, :].rearrange("p (t e) -> p t e", e=8)
            G = gates[:, :].rearrange("p (t e) -> p t e", e=E)
            with nc.Block() as block:
                @block.sync
                def _(sp):
                    sp.dma_start(router[:, :], a["router" if gated else "gate_w1"]).then_inc(small, 16)
                    if gated:
                        sp.dma_start(bias[:, :], a["router_bias"].partition_broadcast(P)).then_inc(small, 16)
                    for i, (n, o) in enumerate(pieces):
                        if i >= 2:
                            sp.wait_ge(lo_made, FROM + i - 1)
                        sp.dma_start(stage[i % 2][:, :], a[n][:, o:o + SC]).then_inc(staged[i % 2], 16)
                    for n in w_down:
                        sp.dma_start(w_down[n][:, :], a[n]).then_inc(downs, 16)
                    if gated:
                        sp.wait_ge(downs, FROM + 16 * len(w_down))

                @block.gpsimd
                def _(pool):
                    for i, (n, o) in enumerate(pieces):
                        pool.wait_ge(staged[i % 2], FROM + 16 * (i // 2 + 1))
                        nc.gpsimd.tensor_copy(w_hi[n][:, o:o + SC], stage[i % 2][:, :]).then_inc(hi_made, 1)
                        pool.wait_ge(hi_made, FROM + i + 1)
                        nc.gpsimd.tensor_tensor(w_lo[n][:, o:o + SC], stage[i % 2][:, :],
                                                w_hi[n][:, o:o + SC].bitcast(F32), ALU.subtract).then_inc(lo_made, 1)

                @block.tensor
                def _(pe):
                    for g in range(GROUPS + 1):
                        if g < GROUPS:
                            pe.wait_ge(rows_ready, FROM + g + 1)
                            if g >= 2:
                                pe.wait_ge(fm_sb, FROM + g - 1)
                            for t in range(TPG):
                                o = (g * TPG + t) * P
                                last = nc.tensor.transpose(ps[g % 2][:, t * P:(t + 1) * P],
                                                           h_tok[:, o:o + P], ident[:, :])
                            last.then_inc(fm_ps, 1)
                        if g:
                            i = g - 1
                            if i == 0:
                                pe.wait_ge(small, FROM + (32 if gated else 16))
                            pe.wait_ge(fm_sb, FROM + i + 1)
                            if i >= 2:
                                pe.wait_ge(logit_sb, FROM + i - 1)
                            for t in range(TPG):
                                last = nc.tensor.matmul(ps[2 + i % 2][:, t * E:(t + 1) * E],
                                                        h_fm[i % 2][:, t * P:(t + 1) * P], router[:, :],
                                                        start=True, stop=True)
                            last.then_inc(logit_ps, 1)
                    if not gated:
                        pe.wait_ge(parts_ready, FROM + 1)
                        for g in range(GROUPS):
                            if g >= 2:
                                pe.wait_ge(gates_sb, FROM + g - 1)
                            for t in range(TPG):
                                o = (g * TPG + t) * 2 * E
                                last = nc.tensor.transpose(ps[g % 2][0:2 * E, t * P:(t + 1) * P],
                                                           gates_2[:, o:o + 2 * E], ident[:, :])
                            last.then_inc(gates_ps, 1)

                @block.scalar
                def _(act):
                    env["norm_act"](act, var_ready, std_ready)
                    for g in range(GROUPS):
                        act.wait_ge(fm_ps, FROM + g + 1)
                        if g >= 2:
                            act.wait_ge(split, FROM + g - 1)
                            act.wait_ge(logit_ps, FROM + g - 1)
                        nc.scalar.activation(h_hi[:, g * GW:(g + 1) * GW], ps[g % 2][:, :], ACT.Copy)
                        nc.scalar.activation(h_fm[g % 2][:, :], ps[g % 2][:, :], ACT.Copy).then_inc(fm_sb, 1)
                    act.wait_ge(shifted, FROM + 1)
                    dst = L[:, :, 0:E] if gated else G
                    nc.scalar.activation(dst, L[:, :, 0:E] if gated else G, ACT.Exp).then_inc(exped, 1)
                    if not gated:
                        for g in range(GROUPS):
                            act.wait_ge(gates_ps, FROM + g + 1)
                            nc.scalar.activation(gates_fm[0:2 * E, g * GW:(g + 1) * GW], ps[g % 2][0:2 * E, :],
                                                 ACT.Copy).then_inc(gates_sb, 1)

                @block.vector
                def _(dve):
                    c = Chain(dve, self_done)
                    env["norm_dve"](dve, c, x_tok, stats_done, var_ready, std_ready)
                    env["norm_rows"](dve, x_tok, h_tok, rows_ready)
                    c.mark(nc.vector.memset(L[:, :, E:LW], outside))
                    c.link(nc.vector.memset(chosen[:, :], outside))
                    dve.wait_ge(small, FROM + (32 if gated else 16))
                    for g in range(GROUPS):
                        dve.wait_ge(fm_sb, FROM + g + 1)
                        o = g * GW
                        nc.vector.tensor_tensor(h_lo[:, o:o + GW], h_fm[g % 2][:, :],
                                                h_hi[:, o:o + GW].bitcast(F32), ALU.subtract).then_inc(split, 1)
                        dve.wait_ge(logit_ps, FROM + g + 1)
                        src = ps[2 + g % 2][:, 0:TPG * E].rearrange("p (t e) -> p t e", e=E)
                        dst = L[:, g * TPG:(g + 1) * TPG, 0:E]
                        if gated:
                            ins = nc.vector.tensor_tensor(dst, src, bias[:, :].unsqueeze(1).broadcast_to(
                                [P, TPG, E]), ALU.add)
                        else:
                            ins = nc.vector.tensor_copy(dst, src)
                        ins.then_inc(logit_sb, 1)
                    dve.wait_ge(logit_sb, FROM + GROUPS)
                    for t in range(TILES):
                        c.mark(nc.vector.max(B[:, t], L[:, t, 0:E]))
                    c.wait()
                    first = B[:, :, 0:1].broadcast_to([P, TILES, E])
                    if gated:
                        nc.vector.tensor_tensor(L[:, :, 0:E], L[:, :, 0:E], first, ALU.subtract).then_inc(shifted, 1)
                        dve.wait_ge(exped, FROM + 1)
                        c.link(nc.vector.tensor_reduce(total[:, :], L[:, :, 0:E], axis=AX.X, op=ALU.add))
                        c.link(nc.vector.reciprocal(total[:, :], total[:, :]))
                        c.link(nc.vector.tensor_tensor(L[:, :, 0:E], L[:, :, 0:E], total[:, :].unsqueeze(
                            2).broadcast_to([P, TILES, E]), ALU.mult))
                        for t in range(TILES):
                            c.mark(nc.vector.max(B[:, t], L[:, t, 0:E]))
                        c.wait()
                    else:
                        nc.vector.tensor_tensor(G, L[:, :, 0:E], first, ALU.subtract).then_inc(shifted, 1)
                    c.link(nc.vector.tensor_copy(C[:, :, 0:K], B[:, :, 0:K]))
                    for t in range(TILES):
                        c.mark(nc.vector.match_replace(R[:, t], C[:, t], L[:, t], 0.0 if gated else -OUTSIDE))
                    c.wait()
                    if gated:
                        c.mark(nc.vector.tensor_tensor(G, L[:, :, 0:E], R[:, :, 0:E], ALU.subtract))
                        c.link(nc.vector.tensor_reduce(total[:, :], B[:, :, 0:K], axis=AX.X, op=ALU.add))
                        c.link(nc.vector.tensor_scalar(total[:, :], total[:, :], 1e-12, None, ALU.max))
                    else:
                        c.link(nc.vector.tensor_tensor(R[:, :, 0:E], L[:, :, 0:E], R[:, :, 0:E], ALU.not_equal))
                        dve.wait_ge(exped, FROM + 1)
                        c.link(nc.vector.tensor_tensor(G, G, R[:, :, 0:E], ALU.mult))
                        c.link(nc.vector.tensor_reduce(total[:, :], G, axis=AX.X, op=ALU.add))
                    c.link(nc.vector.reciprocal(total[:, :], total[:, :]))
                    c.link(nc.vector.tensor_tensor(G, G, total[:, :].unsqueeze(2).broadcast_to([P, TILES, E]), ALU.mult))
                    if not gated:
                        dve.wait_ge(fm_ps, FROM + GROUPS)
                        c.mark(nc.vector.memset(h_tok[:, :], 0.0))
                        c.link(nc.vector.tensor_copy(gates_hi[:, :], gates[:, :]))
                        H = gates_hi[:, :].bitcast(F32).rearrange("p (t e) -> p t e", e=E)
                        G2 = gates_2[:, :].rearrange("p (t e) -> p t e", e=2 * E)
                        c.mark(nc.vector.tensor_copy(G2[:, :, 0:E], H))
                        c.link(nc.vector.tensor_tensor(G2[:, :, E:2 * E], G, H, ALU.subtract))
                        nc.vector.tensor_tensor(
                            selector[:, :].rearrange("p (e m) -> p e m", m=P),
                            ident[:, 0:E].unsqueeze(2).broadcast_to([P, E, P]),
                            ident[:, E:2 * E].unsqueeze(2).broadcast_to([P, E, P]), ALU.add).then_inc(parts_ready, 1)

        if not gated:
            plain_experts(nc, env, pre, h_hi, h_lo, w_hi, w_lo, gates_fm, selector, env["out"])
            return

        with ExitStack() as s:
            def tb(name, cols, dt=F32, rows=P):
                return s.enter_context(nc.sbuf_tensor(pre + name, [rows, cols], dt))
            sem = lambda n: env["semaphore"](pre + n)
            NU = 3
            ps_up = [s.enter_context(nc.psum_tensor(f"{pre}up{i}", [P, GW], F32)) for i in range(NU)]
            ps_gate = [s.enter_context(nc.psum_tensor(f"{pre}gate{i}", [P, GW], F32)) for i in range(NU)] if gated else ps_up
            ps_y = [s.enter_context(nc.psum_tensor(f"{pre}y{i}", [P, GW], F32)) for i in range(2)]
            silu = [tb(f"silu{i}", GW) for i in range(NU)]
            hidden = [tb(f"hidden{i}", GW) for i in range(NU)] if gated else silu
            acc = tb("acc", GW)
            stats, x_stats_done = env["stats"], sem("x_stats_done")
            stats_own, var_ready, std_ready, inverted, normed, x_ready = map(
                sem, ("stats_own", "var_ready", "std_ready", "inverted", "normed", "x_ready"))
            g_now = tb("g_now", TPG * E)
            gate_ps, up_ps, silu_ready, hidden_ready, down_ps, added, acc_self, acc_out = map(
                sem, ("gate_ps", "up_ps", "silu_ready", "hidden_ready", "down_ps", "added", "acc_self", "acc_out"))
            if gated:
                units = [("s", i) for i in range(SH0)] + [("e", i) for i in range(E)]
            else:
                units = [("s", 0)] + [("e", i) for i in range(E)]
            U = len(units)
            steps = U * CH
            hidden_sem = hidden_ready if gated else silu_ready

            def first_weights(kind, i, c):
                if gated:
                    return ("sgate0", "sup0", i * P) if kind == "s" else ("gate0", "up0", i * P)
                return (None, "sw1", c * P) if kind == "s" else (None, "ew1", (i * CH + c) * P)

            def second_weights(kind, i, c):
                if gated:
                    return w_down["sdown0" if kind == "s" else "down0"][:, i * P:(i + 1) * P]
                o = (c if kind == "s" else i * CH + c) * P
                return w_down["sw2" if kind == "s" else "ew2"][:, o:o + P]

            with nc.Block() as block:
                @block.tensor
                def _(pe):
                    with pe.Fori(0, GROUPS) as g:
                        hi, lo = at(h_hi, g * GW, GW), at(h_lo, g * GW, GW)

                        def product(bank, name, o, done):
                            wh, wl = w_hi[name][:, o:o + P], w_lo[name][:, o:o + P]
                            nc.tensor.matmul(bank[:, :], wl, hi, start=True, stop=False)
                            nc.tensor.matmul(bank[:, :], wh, lo, start=False, stop=False)
                            nc.tensor.matmul(bank[:, :], wh, hi, start=False, stop=True).then_inc(done, 1)

                        for n in range(steps + 1):
                            if n < steps:
                                kind, i = units[n // CH]
                                gate, up, o = first_weights(kind, i, n % CH)
                                before = g * steps + (n - NU + 1 if n >= NU - 1 else 0)
                                if gate:
                                    pe.wait_ge(silu_ready, FROM + before)
                                    product(ps_gate[n % NU], gate, o, gate_ps)
                                pe.wait_ge(hidden_sem, FROM + before)
                                product(ps_up[n % NU], up, o, up_ps)
                            if n:
                                m = n - 1
                                (kind, i), c = units[m // CH], m % CH
                                pe.wait_ge(hidden_sem, FROM + g * steps + m + 1)
                                if c == 0:
                                    u = m // CH
                                    pe.wait_ge(added, FROM + (g * U + (u - 1 if u else 0)))
                                for t in range(TPG):
                                    last = nc.tensor.matmul(
                                        ps_y[m // CH % 2][:, t * P:(t + 1) * P],
                                        hidden[m % NU][:, t * P:(t + 1) * P], second_weights(kind, i, c),
                                        start=(c == 0 and t == 0), stop=(c == CH - 1), skip_group_check=True)
                                last.then_inc(down_ps, 1)

                @block.scalar
                def _(act):
                    def group(g, first):
                        for n in range(steps):
                            if n == 9 and not first:
                                env["residual_std"](act, g - 1, var_ready, std_ready)
                            if gated:
                                act.wait_ge(gate_ps, FROM + g * steps + n + 1)
                                before = g * steps + (n - NU + 1 if n >= NU - 1 else 0)
                                act.wait_ge(hidden_ready, FROM + before)
                                nc.scalar.activation(silu[n % NU][:, :], ps_gate[n % NU][:, :],
                                                     ACT.Silu).then_inc(silu_ready, 1)

                    groups(act, group)
                    env["residual_std"](act, GROUPS - 1, var_ready, std_ready)

                @block.vector
                def _(dve):
                    def group_stats(g):
                        dve.wait_ge(acc_out, FROM + g + 1)
                        env["residual_stats"](dve, stats_own, g, at(y_tok, g * GW, GW), var_ready)

                    def x_stats(g):
                        dve.wait_ge(x_ready, FROM + g + 1)
                        for t in range(TPG):
                            nc.vector.bn_stats(at(stats, g * (TPG * 6) + t * 6, 6),
                                               at(x_tok, g * GW + t * P)).then_inc(x_stats_done, 1)

                    def group_norm(g):
                        env["residual_norm"](dve, g, at(y_tok, g * GW, GW), std_ready, inverted, normed)

                    def group(g, first):
                        c = Chain(dve, acc_self, g)
                        c.link(nc.vector.tensor_copy(g_now[:, :], at(gates, g * (TPG * E), TPG * E)))
                        for n in range(U + 1):
                            if n == 8 and not first:
                                group_stats(g - 1)
                            if n == 11 and not first:
                                group_norm(g - 1)
                            if n == 16 and not first:
                                x_stats(g - 1)
                            if gated and n < U:
                                dve.wait_ge(silu_ready, FROM + g * steps + n + 1)
                                dve.wait_ge(up_ps, FROM + g * steps + n + 1)
                                dve.wait_ge(down_ps, FROM + g * steps + max(n - NU + 1, 0))
                                nc.vector.tensor_tensor(hidden[n % NU][:, :], ps_up[n % NU][:, :],
                                                        silu[n % NU][:, :], ALU.mult).then_inc(hidden_ready, 1)
                            if n:
                                u = n - 1
                                kind, i = units[u]
                                y = ps_y[u % 2]
                                dve.wait_ge(down_ps, FROM + g * steps + (u + 1) * CH)
                                if u == 0:
                                    dve.wait_ge(acc_out, FROM + g)
                                    last = nc.vector.tensor_copy(acc[:, :], y[:, :])
                                elif kind == "s":
                                    last = nc.vector.tensor_tensor(acc[:, :], y[:, :], acc[:, :], ALU.add)
                                else:
                                    for t in range(TPG):
                                        cols = slice(t * P, (t + 1) * P)
                                        last = nc.vector.scalar_tensor_tensor(
                                            acc[:, cols], y[:, cols], g_now[:, t * E + i:t * E + i + 1],
                                            acc[:, cols], ALU.mult, ALU.add)
                                last.then_inc(added, 1)
                                dve.wait_ge(added, FROM + g * U + u + 1)

                    groups(dve, group)
                    group_stats(GROUPS - 1)
                    group_norm(GROUPS - 1)
                    x_stats(GROUPS - 1)
                    dve.wait_ge(x_stats_done, FROM + TILES)

                @block.gpsimd
                def _(pool):
                    def group(g, first):
                        if not first:
                            env["residual_add"](pool, g - 1, normed, x_ready)
                        pool.wait_ge(added, FROM + (g + 1) * U)
                        nc.gpsimd.tensor_copy(at(y_tok, g * GW, GW), acc[:, :]).then_inc(acc_out, 1)

                    groups(pool, group)
                    env["residual_add"](pool, GROUPS - 1, normed, x_ready)


def plain_experts(nc, env, pre, h_hi, h_lo, w_hi, w_lo, gates_fm, selector, out):
    x_tok, y_tok, ident = env["x_tok"], env["y_tok"], env["ident"]
    units = [("s", 0)] + [("e", i) for i in range(E1)]
    steps = len(units) * CH1
    scaled_steps = E1 * CH1
    NU = 4
    LAG = 3
    with ExitStack() as s:
        def tb(name, cols, dt=F32, rows=P):
            return s.enter_context(nc.sbuf_tensor(pre + name, [rows, cols], dt))
        sem = lambda n: env["semaphore"](pre + n)
        ps_up = [s.enter_context(nc.psum_tensor(f"{pre}up{i}", [P, GW], F32)) for i in range(NU)]
        ps_gates = [s.enter_context(nc.psum_tensor(f"{pre}gates{i}", [P, GW], F32)) for i in range(2)]
        ps_y = s.enter_context(nc.psum_tensor(f"{pre}y", [P, GW], F32))
        ps_rows = s.enter_context(nc.psum_tensor(f"{pre}rows", [P, GW], F32))
        silu = [tb(f"silu{i}", GW) for i in range(NU)]
        hid_hi, hid_lo = ([tb(f"{n}{i}", GW, F32R) for i in range(NU)] for n in ("hid_hi", "hid_lo"))
        y_fm = tb("y_fm", GW)
        gates_now = tb("gates_now", GW, F32R)
        gates_ps, up_ps, silu_ready, scaled, hi_ready, lo_ready, down_ps, y_fm_ready, rows_ps, rows_out = map(
            sem, ("spread_ps", "up_ps", "silu_ready", "scaled", "hi_ready", "lo_ready", "down_ps", "y_fm_ready",
                  "rows_ps", "rows_out"))
        now_ready = sem("now_ready")
        stats_done, stats_own, var_ready, std_ready, normed, x_ready, stored = map(
            sem, ("stats_done", "stats_own", "var_ready", "std_ready", "normed", "x_ready", "stored"))
        stats, mean, rstd, spread = env["stats"], env["mean"], env["rstd"], env["spread"]

        def columns(n, first):
            kind, i = units[n // CH1]
            if kind == "s":
                return "sw1" if first else "sw2", n % CH1 * P
            return "ew1" if first else "ew2", (i * CH1 + n % CH1) * P

        def three_products(bank, name, o, hi, lo, start, stop):
            wh, wl = w_hi[name][:, o:o + P], w_lo[name][:, o:o + P]
            nc.tensor.matmul(bank[:, :], wl, hi, start=start, stop=False)
            nc.tensor.matmul(bank[:, :], wh, lo, start=False, stop=False)
            return nc.tensor.matmul(bank[:, :], wh, hi, start=False, stop=stop)

        with nc.Block() as block:
            @block.tensor
            def _(pe):
                def second(g, m):
                    pe.wait_ge(lo_ready, FROM + g * steps + m + 1)
                    three_products(ps_y, *columns(m, False), hid_hi[m % NU][:, :], hid_lo[m % NU][:, :],
                                   m == 0, m == steps - 1).then_inc(down_ps, 1)

                def rows(g):
                    pe.wait_ge(y_fm_ready, FROM + g + 1)
                    pe.wait_ge(rows_out, FROM + g)
                    for t in range(TPG):
                        last = nc.tensor.transpose(ps_rows[:, t * P:(t + 1) * P], y_fm[:, t * P:(t + 1) * P], ident[:, :])
                    last.then_inc(rows_ps, 1)

                def group(g, first):
                    hi, lo = at(h_hi, g * GW, GW), at(h_lo, g * GW, GW)
                    for n in range(steps):
                        kind, i = units[n // CH1]
                        if kind == "e" and n % CH1 == 0:
                            pe.wait_ge(scaled, FROM + g * scaled_steps + max(i - 1, 0) * CH1)
                            pe.wait_ge(now_ready, FROM + g + 1)
                            nc.tensor.matmul(ps_gates[i % 2][:, :], selector[:, i * P:(i + 1) * P],
                                             gates_now[:, :], start=True, stop=True).then_inc(gates_ps, 1)
                        pe.wait_ge(silu_ready, FROM + g * steps + max(n - NU + 1, 0))
                        three_products(ps_up[n % NU], *columns(n, True), hi, lo, True, True).then_inc(up_ps, 1)
                        if n >= LAG:
                            if n == LAG:
                                pe.wait_ge(y_fm_ready, FROM + g)
                            second(g, n - LAG)
                        elif not first:
                            second(g - 1, steps + n - LAG)
                        if n == LAG + 2 and not first:
                            rows(g - 1)

                groups(pe, group)
                for m in range(steps - LAG, steps):
                    second(GROUPS - 1, m)
                rows(GROUPS - 1)

            @block.scalar
            def _(act):
                def sum_out(g):
                    act.wait_ge(down_ps, FROM + (g + 1) * steps)
                    act.wait_ge(rows_ps, FROM + g)
                    nc.scalar.activation(y_fm[:, :], ps_y[:, :], ACT.Copy).then_inc(y_fm_ready, 1)

                def group(g, first):
                    for n in range(steps + 1):
                        if n == LAG and not first:
                            sum_out(g - 1)
                        if n < steps:
                            act.wait_ge(up_ps, FROM + g * steps + n + 1)
                            act.wait_ge(lo_ready, FROM + g * steps + max(n - NU + 1, 0))
                            nc.scalar.activation(silu[n % NU][:, :], ps_up[n % NU][:, :],
                                                 ACT.Silu).then_inc(silu_ready, 1)
                        if n:
                            m = n - 1
                            if m < CH1:
                                act.wait_ge(silu_ready, FROM + g * steps + m + 1)
                            else:
                                act.wait_ge(scaled, FROM + g * scaled_steps + m - CH1 + 1)
                            act.wait_ge(down_ps, FROM + g * steps + max(m - NU + 1, 0))
                            nc.scalar.activation(hid_hi[m % NU][:, :], silu[m % NU][:, :],
                                                 ACT.Copy).then_inc(hi_ready, 1)

                groups(act, group)
                sum_out(GROUPS - 1)
                env["norm_act"](act, var_ready, std_ready)

            @block.vector
            def _(dve):
                def rows(g):
                    dve.wait_ge(rows_ps, FROM + g + 1)
                    nc.vector.tensor_copy(at(y_tok, g * GW, GW), ps_rows[:, :]).then_inc(rows_out, 1)

                def row_stats(g, t):
                    dve.wait_ge(rows_out, FROM + g + 1)
                    nc.vector.bn_stats(at(stats, g * (TPG * 6) + t * 6, 6),
                                       at(y_tok, g * GW + t * P)).then_inc(stats_done, 1)

                def group(g, first):
                    dve.wait_ge(gates_ps, FROM + g * E1)
                    nc.vector.tensor_copy(gates_now[:, :], at(gates_fm, g * GW, GW)).then_inc(now_ready, 1)
                    for n in range(CH1, steps):
                        if n == 2 * CH1 and not first:
                            rows(g - 1)
                        if n % CH1 == 2 and 2 <= n // CH1 < 2 + TPG and not first:
                            row_stats(g - 1, n // CH1 - 2)
                        dve.wait_ge(silu_ready, FROM + g * steps + n + 1)
                        if n % CH1 == 0:
                            dve.wait_ge(gates_ps, FROM + g * E1 + n // CH1)
                        nc.vector.tensor_tensor(silu[n % NU][:, :], ps_gates[(n // CH1 - 1) % 2][:, :],
                                                silu[n % NU][:, :], ALU.mult).then_inc(scaled, 1)

                groups(dve, group)
                rows(GROUPS - 1)
                for t in range(TPG):
                    row_stats(GROUPS - 1, t)
                dve.wait_ge(stats_done, FROM + TILES)
                c = Chain(dve, stats_own)
                env["merge_stats"](c, stats[:, :], mean[:, :], rstd[:, :], spread[:, :], P // 2)
                dve.sem_inc(var_ready, 1)
                dve.wait_ge(std_ready, FROM + 1)
                c.link(nc.vector.reciprocal(rstd[:, :], rstd[:, :]))
                env["norm_rows"](dve, y_tok, y_tok, normed)

            @block.gpsimd
            def _(pool):
                def group(g, first):
                    for m in range(steps):
                        pool.wait_ge(hi_ready, FROM + g * steps + m + 1)
                        pool.wait_ge(down_ps, FROM + g * steps + max(m - NU + 1, 0))
                        nc.gpsimd.tensor_tensor(hid_lo[m % NU][:, :], silu[m % NU][:, :],
                                                hid_hi[m % NU][:, :].bitcast(F32), ALU.subtract).then_inc(lo_ready, 1)

                groups(pool, group)
                with pool.Fori(0, GROUPS) as g:
                    env["residual_add"](pool, g, normed, x_ready)

            @block.sync
            def _(sp):
                for g in range(GROUPS):
                    sp.wait_ge(x_ready, FROM + g + 1)
                    sp.dma_start(out[g * BPG:(g + 1) * BPG].rearrange("b (u p) c -> p b u c", p=P),
                                 x_tok[:, g * GW:(g + 1) * GW].rearrange(
                                     "p (b u c) -> p b u c", u=TPB, c=P)).then_inc(stored, 16)
                sp.wait_ge(stored, FROM + 16 * GROUPS)


def rwkv(nc, a, env):
    x_tok, y_tok, h_tok, ident = env["x_tok"], env["y_tok"], env["h_tok"], env["ident"]
    W1T = T + 1
    phase = ExitStack()
    with phase:
        def sb(name, cols, dt=F32, rows=P):
            return phase.enter_context(nc.sbuf_tensor("c_" + name, [rows, cols], dt))

        mats = {n: sb(n, P) for n in ("att_Wk", "att_Wv", "att_Wr", "att_Wo", "ffn_Wr")}
        mats["ffn_Wk"] = sb("ffn_Wk", CH_RWKV * P)
        mats["ffn_Wv"] = sb("ffn_Wv", CH_RWKV * P)
        NVEC = ("ln1_g", "ln1_b", "ln2_g", "ln2_b", "time_decay", "time_first", "time_mix_k", "time_mix_v",
                "time_mix_r", "cm_k", "cm_r")
        vec = {n: sb(n, 1) for n in NVEC}
        rest_of = {n: sb(n + "_rest", 1) for n in ("time_mix_k", "time_mix_v", "time_mix_r", "cm_k", "cm_r")}
        decay = sb("decay", 1)

        def load_norm_transpose(tag, src, to_h, gname, bname, dst, first):
            with ExitStack() as s:
                sem = lambda n: env["semaphore"](tag + n)
                ps = [s.enter_context(nc.psum_tensor(f"{tag}ps{i}", [P, GW], F32)) for i in range(2)]
                loaded, derived = sem("loaded"), sem("derived")
                sems = [tuple(map(sem, (f"stats{i}", f"dve{i}", f"var{i}", f"std{i}", f"rows{i}"))) for i in range(2)]
                fm_ps, fm_sb = sem("fm_ps"), sem("fm_sb")
                NL = 16 * (len(mats) + len(vec))
                with nc.Block() as block:
                    if first:
                        @block.sync
                        def _(sp):
                            for n in vec:
                                sp.dma_start(vec[n][:, :], a[n]).then_inc(loaded, 16)
                            for n in mats:
                                sp.dma_start(mats[n][:, :], a[n]).then_inc(loaded, 16)
                            sp.wait_ge(loaded, FROM + NL)

                    @block.vector
                    def _(dve):
                        d3 = dst[:, :].rearrange("p (b t) -> p b t", t=W1T)
                        nc.vector.memset(d3[:, :, 0:1], 0.0)
                        if to_h:
                            st, own, var, std, rows = sems[0]
                            env["norm_dve"](dve, Chain(dve, own), None, st, var, std)
                            env["norm_rows"](dve, src, h_tok, rows)
                            dve.wait_ge(rows, FROM + GROUPS)
                        st, own, var, std, rows = sems[1]
                        env["norm_dve"](dve, Chain(dve, own), h_tok, st, var, std)
                        env["norm_rows"](dve, h_tok, y_tok, rows)
                        if first:
                            dve.wait_ge(loaded, FROM + NL)
                            for n in rest_of:
                                nc.vector.tensor_scalar(rest_of[n][:, :], vec[n][:, :], -1.0, 1.0, ALU.mult, ALU.add)
                            dve.wait_ge(derived, FROM + 1)
                            nc.vector.tensor_scalar(decay[:, :], decay[:, :], -1.0, None, ALU.mult)

                    @block.scalar
                    def _(act):
                        if to_h:
                            env["norm_act"](act, sems[0][2], sems[0][3])
                        env["norm_act"](act, sems[1][2], sems[1][3])
                        if first:
                            act.wait_ge(loaded, FROM + NL)
                            nc.scalar.activation(decay[:, :], vec["time_decay"][:, :], ACT.Exp).then_inc(derived, 1)
                        for g in range(GROUPS):
                            act.wait_ge(fm_ps, FROM + g + 1)
                            o = g * BPG * W1T
                            nc.scalar.activation(
                                dst[:, o:o + BPG * W1T].rearrange("p (b t) -> p b t", t=W1T)[:, :, 1:W1T],
                                ps[g % 2][:, :].rearrange("p (b t) -> p b t", t=T), ACT.Identity,
                                bias=vec[bname][:, :], scale=vec[gname][:, :]).then_inc(fm_sb, 1)

                    @block.tensor
                    def _(pe):
                        env["transposes"](pe, y_tok, ps, sems[1][4], fm_ps, fm_sb)

        def mixed(c, src, g, name, tmp, dst):
            s3 = at(src, g * (BPG * W1T), BPG * W1T).rearrange("p (b t) -> p b t", t=W1T)
            t3 = tmp[:, :].rearrange("p (b t) -> p b t", t=T)
            d3 = dst[:, :].rearrange("p (b t) -> p b t", t=T)
            c.link(nc.vector.tensor_scalar(t3, s3[:, :, 0:T], rest_of[name][:, :], None, ALU.mult))
            return nc.vector.scalar_tensor_tensor(d3, s3[:, :, 1:W1T], vec[name][:, :], t3, ALU.mult, ALU.add)

        with ExitStack() as rkv:
            k_all, v_all, r_all = (rkv.enter_context(nc.sbuf_tensor(n, [P, N], F32)) for n in ("k_all", "v_all", "r_all"))

            with ExitStack() as s:
                def tb(name, cols, dt=F32, rows=P):
                    return s.enter_context(nc.sbuf_tensor(name, [rows, cols], dt))
                xa = tb("xa", NB * W1T)
                load_norm_transpose("c1_", x_tok, True, "ln1_g", "ln1_b", xa, True)
                sem = lambda n: env["semaphore"]("c2_" + n)
                names = ("k", "v", "r")
                mix = {n: tb("mix_" + n, GW) for n in names}
                tmp = {n: tb("mix_tmp_" + n, GW) for n in names}
                ps = {n: [s.enter_context(nc.psum_tensor(f"c2_ps_{n}{i}", [P, GW], F32)) for i in range(2)] for n in names}
                mix_ready = {n: sem("mix_" + n) for n in names}
                out_ps = {n: sem("ps_" + n) for n in names}
                out_sb = {n: sem("sb_" + n) for n in names}
                own = sem("dve_done")
                with nc.Block() as block:
                    @block.vector
                    def _(dve):
                        with dve.Fori(0, GROUPS) as g:
                            c = Chain(dve, own, g * 3)
                            for n in names:
                                dve.wait_ge(out_ps[n], FROM + g)
                                mixed(c, xa, g, "time_mix_" + n, tmp[n], mix[n]).then_inc(mix_ready[n], 1)

                    @block.tensor
                    def _(pe):
                        with pe.Fori(0, GROUPS // 2) as g2:
                            for u in range(2):
                                for n in names:
                                    pe.wait_ge(mix_ready[n], FROM + g2 * 2 + u + 1)
                                    pe.wait_ge(out_sb[n], FROM + g2 * 2)
                                    nc.tensor.matmul(ps[n][u][:, :], mats["att_W" + n][:, :], mix[n][:, :],
                                                     start=True, stop=True).then_inc(out_ps[n], 1)

                    @block.scalar
                    def _(act):
                        with act.Fori(0, GROUPS // 2) as g2:
                            for u in range(2):
                                for n, dst in zip(names, (k_all, v_all, r_all)):
                                    act.wait_ge(out_ps[n], FROM + g2 * 2 + u + 1)
                                    nc.scalar.activation(at(dst, g2 * (2 * GW) + u * GW, GW), ps[n][u][:, :],
                                                         ACT.Sigmoid if n == "r" else ACT.Copy).then_inc(out_sb[n], 1)

            with ExitStack() as s:
                def tb(name, cols, dt=F32, rows=P):
                    return s.enter_context(nc.sbuf_tensor("s_" + name, [rows, cols], dt))
                sem = lambda n: env["semaphore"]("c3_" + n)
                w_row = tb("w_row", T)
                peak = [tb(f"peak{i}", BPG * W1T) for i in range(2)]
                peak_out = [tb(f"peak_out{i}", GW) for i in range(2)]
                KINDS = 4
                ex = tb("ex", GROUPS * KINDS * GW)
                new_v = [tb(f"new_v{i}", GW) for i in range(2)]
                out_v = [tb(f"out_v{i}", GW) for i in range(2)]
                a_st, b_st = tb("a_st", BPG * W1T), tb("b_st", BPG * W1T)
                num, den = tb("num", GW), tb("den", GW)
                wkv = [tb(f"wkv{i}", GW) for i in range(2)]
                ps = [s.enter_context(nc.psum_tensor(f"c3_ps{i}", [P, GW], F32)) for i in range(2)]
                peaks = sem("peaks")
                pool_diffs = sem("pool_diffs")
                own1, own2, diffs, exped, vs_ready, vs_used, wkv_ready, wo_ps, wo_sb = map(
                    sem, ("own1", "own2", "diffs", "exped", "vs_ready", "vs_used", "wkv_ready", "wo_ps", "wo_sb"))

                def b3(x, n=T):
                    return x.rearrange("p (b t) -> p b t", t=n)

                with nc.Block() as block:
                    @block.vector
                    def _(dve):
                        own0 = own1
                        c = Chain(dve, own0)
                        c.mark(nc.vector.memset(w_row[:, :], 0.0))
                        for i in range(2):
                            c.mark(nc.vector.memset(b3(peak[i][:, :], W1T)[:, :, 0:1], NEVER))
                        c.mark(nc.vector.memset(b3(a_st[:, :], W1T)[:, :, 0:1], 0.0))
                        c.link(nc.vector.memset(b3(b_st[:, :], W1T)[:, :, 0:1], 0.0))
                        c.link(nc.vector.tensor_scalar(w_row[:, :], w_row[:, :], decay[:, :], None, ALU.add))
                        start, steps = c.n, 3
                        u_ = vec["time_first"][:, :]
                        dve.sem_inc(pool_diffs, 1)
                        with dve.Fori(0, GROUPS // 2) as g2:
                            for u in range(2):
                                g = g2 * 2 + u
                                c = Chain(dve, own1, start + g * steps)
                                dve.wait_ge(pool_diffs, FROM + g)
                                for i in range(BPG):
                                    c.mark(nc.vector.tensor_tensor_scan(
                                        peak[u][:, i * W1T + 1:(i + 1) * W1T], w_row[:, :],
                                        at(k_all, g2 * (2 * GW) + u * GW + i * T, T), NEVER, ALU.add, ALU.max))
                                k3 = b3(at(k_all, g2 * (2 * GW) + u * GW, GW))
                                was, now = b3(peak[u][:, :], W1T)[:, :, 0:T], b3(peak[u][:, :], W1T)[:, :, 1:W1T]
                                c.wait()
                                e = [b3(at(ex, g2 * (2 * KINDS * GW) + (u * KINDS + i) * GW, GW)) for i in range(KINDS)]
                                c.link(nc.vector.scalar_tensor_tensor(b3(peak_out[u][:, :]), k3, u_, was,
                                                                      ALU.add, ALU.max))
                                dve.sem_inc(peaks, 1)
                                nc.vector.scalar_tensor_tensor(e[0], was, decay[:, :], now, ALU.add, ALU.subtract)
                                nc.vector.scalar_tensor_tensor(e[3], k3, u_, b3(peak_out[u][:, :]), ALU.add,
                                                               ALU.subtract).then_inc(diffs, 1)
                        steps = 7

                        def output(g, u):
                            c = Chain(dve, own2, g * steps)
                            dve.wait_ge(vs_ready, FROM + g + 1)
                            e = [at(ex, g * (KINDS * GW) + i * GW, GW) for i in range(KINDS)]
                            for i in range(BPG):
                                cols = slice(i * T, (i + 1) * T)
                                c.mark(nc.vector.tensor_tensor_scan(
                                    a_st[:, i * W1T + 1:(i + 1) * W1T], e[0][:, cols], new_v[u][:, cols],
                                    0.0, ALU.mult, ALU.add))
                                c.mark(nc.vector.tensor_tensor_scan(
                                    b_st[:, i * W1T + 1:(i + 1) * W1T], e[0][:, cols], e[1][:, cols],
                                    0.0, ALU.mult, ALU.add))
                            c.wait()
                            n3, d3 = b3(num[:, :]), b3(den[:, :])
                            nc.vector.tensor_tensor(n3, b3(e[2]), b3(a_st[:, :], W1T)[:, :, 0:T], ALU.mult)
                            c.link(nc.vector.tensor_tensor(d3, b3(e[2]), b3(b_st[:, :], W1T)[:, :, 0:T], ALU.mult))
                            nc.vector.tensor_tensor(num[:, :], num[:, :], out_v[u][:, :], ALU.add).then_inc(vs_used, 1)
                            c.link(nc.vector.tensor_tensor(den[:, :], den[:, :], e[3], ALU.add))
                            nc.vector.tensor_tensor(num[:, :], num[:, :], at(r_all, g * GW, GW), ALU.mult)
                            c.link(nc.vector.reciprocal(den[:, :], den[:, :]))
                            nc.vector.tensor_tensor(wkv[u][:, :], num[:, :], den[:, :], ALU.mult).then_inc(wkv_ready, 1)
                            assert c.n == steps, c.n

                        def step(g, u):
                            if not is_at(g, GROUPS):
                                output(g, u)
                            if not is_at(g, 0):
                                dve.wait_ge(wo_ps, FROM + g)
                                h = at(h_tok, (g - 1) * GW, GW)
                                nc.vector.tensor_tensor(h, ps[1 - u][:, :], h, ALU.add).then_inc(wo_sb, 1)
                        pipelined(dve, GROUPS, step)

                    @block.scalar
                    def _(act):
                        with act.Fori(0, GROUPS) as g:
                            act.wait_ge(diffs, FROM + g + 1)
                            act.wait_ge(pool_diffs, FROM + g + 2)
                            e = at(ex, g * (KINDS * GW), KINDS * GW)
                            nc.scalar.activation(e, e, ACT.Exp).then_inc(exped, 1)

                    @block.gpsimd
                    def _(pool):
                        with pool.Fori(0, GROUPS // 2) as g2:
                            for u in range(2):
                                pool.wait_ge(peaks, FROM + g2 * 2 + u + 1)
                                e = [b3(at(ex, g2 * (2 * KINDS * GW) + (u * KINDS + i) * GW, GW)) for i in range(KINDS)]
                                nc.gpsimd.tensor_tensor(e[1], b3(at(k_all, g2 * (2 * GW) + u * GW, GW)),
                                                        b3(peak[u][:, :], W1T)[:, :, 1:W1T], ALU.subtract)
                                nc.gpsimd.tensor_tensor(e[2], b3(peak[u][:, :], W1T)[:, :, 0:T],
                                                        b3(peak_out[u][:, :]), ALU.subtract).then_inc(pool_diffs, 1)
                        with pool.Fori(0, GROUPS // 2) as g2:
                            for u in range(2):
                                pool.wait_ge(exped, FROM + g2 * 2 + u + 1)
                                pool.wait_ge(vs_used, FROM + g2 * 2)
                                v = at(v_all, g2 * (2 * GW) + u * GW, GW)
                                e = [at(ex, g2 * (2 * KINDS * GW) + (u * KINDS + i) * GW, GW) for i in range(KINDS)]
                                nc.gpsimd.tensor_tensor(new_v[u][:, :], e[1], v, ALU.mult)
                                nc.gpsimd.tensor_tensor(out_v[u][:, :], e[3], v, ALU.mult).then_inc(vs_ready, 1)

                    @block.tensor
                    def _(pe):
                        with pe.Fori(0, GROUPS // 2) as g2:
                            for u in range(2):
                                pe.wait_ge(wkv_ready, FROM + g2 * 2 + u + 1)
                                pe.wait_ge(wo_sb, FROM + g2 * 2)
                                for t in range(TPG):
                                    last = nc.tensor.matmul(ps[u][:, t * P:(t + 1) * P], wkv[u][:, t * P:(t + 1) * P],
                                                            mats["att_Wo"][:, :], start=True, stop=True)
                                last.then_inc(wo_ps, 1)

        with ExitStack() as s:
            def tb(name, cols, dt=F32, rows=P):
                return s.enter_context(nc.sbuf_tensor("f_" + name, [rows, cols], dt))
            xc = tb("xc", NB * W1T)
            load_norm_transpose("c4_", None, False, "ln2_g", "ln2_b", xc, False)
            sem = lambda n: env["semaphore"]("c5_" + n)
            mix_k, mix_r = ([tb(f"{n}{i}", GW) for i in range(2)] for n in ("mix_k", "mix_r"))
            tmp_k, tmp_r = tb("tmp_k", GW), tb("tmp_r", GW)
            kk = [[tb(f"kk{i}_{c}", GW) for c in range(CH_RWKV)] for i in range(2)]
            sig, prod = ([tb(f"{n}{i}", GW) for i in range(2)] for n in ("sig", "prod"))
            ps_k = [s.enter_context(nc.psum_tensor(f"c5_k{i}", [P, GW], F32)) for i in range(CH_RWKV)]
            ps_r = s.enter_context(nc.psum_tensor("c5_r", [P, GW], F32))
            ps_v = [s.enter_context(nc.psum_tensor(f"c5_v{i}", [P, GW], F32)) for i in range(2)]
            first = [tb(f"first{i}", GW) for i in range(CH_RWKV)]
            stats, stats_done = env["stats"], sem("stats_done")
            own, mix_ready, k_ps, k_sb, kk_ready, r_ps, r_sb, v_ps, prod_ready, y_out = map(
                sem, ("own", "mix_ready", "k_ps", "k_sb", "kk_ready", "r_ps", "r_sb", "v_ps", "prod_ready", "y_out"))
            with nc.Block() as block:
                @block.vector
                def _(dve):
                    def mix(g, u):
                        c = Chain(dve, own, g * 2)
                        if not (is_at(g, 0) or is_at(g, 1)):
                            dve.wait_ge(r_ps, FROM + g - 1)
                        mixed(c, xc, g, "cm_k", tmp_k, mix_k[u])
                        mixed(c, xc, g, "cm_r", tmp_r, mix_r[u]).then_inc(mix_ready, 1)

                    def step(g, u):
                        if is_at(g, 0):
                            mix(0, 0)
                        if not (is_at(g, GROUPS - 1) or is_at(g, GROUPS)):
                            mix(g + 1, 1 - u)
                        if not is_at(g, GROUPS):
                            if not (is_at(g, 0) or is_at(g, 1)):
                                dve.wait_ge(v_ps, FROM + g - 1)
                            for i in range(CH_RWKV):
                                dve.wait_ge(k_sb, FROM + g * CH_RWKV + i + 1)
                                nc.vector.scalar_tensor_tensor(
                                    kk[u][i][:, :], first[i][:, :], 0.0, first[i][:, :],
                                    ALU.max, ALU.mult).then_inc(kk_ready, 1)
                        if not is_at(g, 0):
                            dve.wait_ge(r_sb, FROM + g)
                            dve.wait_ge(v_ps, FROM + g)
                            nc.vector.tensor_tensor(prod[1 - u][:, :], ps_v[1 - u][:, :], sig[1 - u][:, :],
                                                    ALU.mult).then_inc(prod_ready, 1)
                            dve.wait_ge(y_out, FROM + g)
                            for t in range(TPG):
                                nc.vector.bn_stats(at(stats, (g - 1) * (TPG * 6) + t * 6, 6),
                                                   at(y_tok, (g - 1) * GW + t * P)).then_inc(stats_done, 1)
                    pipelined(dve, GROUPS, step)
                    dve.wait_ge(stats_done, FROM + TILES)

                @block.tensor
                def _(pe):
                    def step(g, u):
                        if not is_at(g, GROUPS):
                            pe.wait_ge(mix_ready, FROM + g + 1)
                            for i in range(CH_RWKV):
                                pe.wait_ge(k_sb, FROM + g * CH_RWKV)
                                nc.tensor.matmul(ps_k[i][:, :], mats["ffn_Wk"][:, i * P:(i + 1) * P],
                                                 mix_k[u][:, :], start=True, stop=True).then_inc(k_ps, 1)
                            pe.wait_ge(r_sb, FROM + g)
                            for t in range(TPG):
                                last = nc.tensor.matmul(ps_r[:, t * P:(t + 1) * P], mix_r[u][:, t * P:(t + 1) * P],
                                                        mats["ffn_Wr"][:, :], start=True, stop=True)
                            last.then_inc(r_ps, 1)
                        if not is_at(g, 0):
                            pe.wait_ge(prod_ready, FROM + g - 1)
                            for i in range(CH_RWKV):
                                pe.wait_ge(kk_ready, FROM + (g - 1) * CH_RWKV + i + 1)
                                for t in range(TPG):
                                    last = nc.tensor.matmul(
                                        ps_v[1 - u][:, t * P:(t + 1) * P], kk[1 - u][i][:, t * P:(t + 1) * P],
                                        mats["ffn_Wv"][:, i * P:(i + 1) * P], start=(i == 0 and t == 0),
                                        stop=(i == CH_RWKV - 1), skip_group_check=True)
                            last.then_inc(v_ps, 1)
                    pipelined(pe, GROUPS, step)

                @block.scalar
                def _(act):
                    with act.Fori(0, GROUPS // 2) as g2:
                        for u in range(2):
                            for i in range(CH_RWKV):
                                act.wait_ge(k_ps, FROM + g2 * (2 * CH_RWKV) + u * CH_RWKV + i + 1)
                                act.wait_ge(kk_ready, FROM + g2 * (2 * CH_RWKV) + u * CH_RWKV)
                                nc.scalar.activation(first[i][:, :], ps_k[i][:, :], ACT.Copy).then_inc(k_sb, 1)
                            act.wait_ge(r_ps, FROM + g2 * 2 + u + 1)
                            act.wait_ge(prod_ready, FROM + g2 * 2)
                            nc.scalar.activation(sig[u][:, :], ps_r[:, :], ACT.Sigmoid).then_inc(r_sb, 1)

                @block.gpsimd
                def _(pool):
                    with pool.Fori(0, GROUPS // 2) as g2:
                        for u in range(2):
                            pool.wait_ge(prod_ready, FROM + g2 * 2 + u + 1)
                            o = g2 * (2 * GW) + u * GW
                            nc.gpsimd.tensor_tensor(at(y_tok, o, GW), prod[u][:, :], at(h_tok, o, GW),
                                                    ALU.add).then_inc(y_out, 1)


def laid_out(d):
    f = lambda n: np.asarray(d[n])
    c = np.ascontiguousarray
    w = {"x": f("L0_attn_hidden_states")}
    for n in ("Wq", "Wk", "Wv", "W1", "W2"):
        w[n] = f("L0_attn_" + n)
    for n in ("bq", "bk", "bv", "b1", "b2"):
        w[n] = f("L0_attn_" + n).reshape(-1, 1)
    w["router"] = f("L0_ffn_router_w").T
    w["router_bias"] = f("L0_ffn_router_bias").reshape(1, -1)
    w["gate0"] = f("L0_ffn_gate_w").transpose(2, 0, 1).reshape(P, -1)
    w["up0"] = f("L0_ffn_up_w").transpose(2, 0, 1).reshape(P, -1)
    w["down0"] = f("L0_ffn_down_w").transpose(2, 0, 1).reshape(P, -1)
    w["sgate0"] = f("L0_ffn_sgate_w").T
    w["sup0"] = f("L0_ffn_sup_w").T
    w["sdown0"] = f("L0_ffn_sdown_w").T.reshape(SH0, P, P).transpose(1, 0, 2).reshape(P, -1)
    for n in ("ln1_g", "ln1_b", "ln2_g", "ln2_b", "time_decay", "time_first", "time_mix_k", "time_mix_v",
              "time_mix_r", "cm_k", "cm_r"):
        w[n] = f("L1_attn_" + n).reshape(P, 1)
    for n in ("att_Wk", "att_Wv", "att_Wr", "att_Wo", "ffn_Wk", "ffn_Wr"):
        w[n] = f("L1_attn_" + n).T
    w["ffn_Wv"] = f("L1_attn_ffn_Wv").T.reshape(CH_RWKV, P, P).transpose(1, 0, 2).reshape(P, -1)
    w["gate_w1"] = f("L1_ffn_gate_w").T
    w["sw1"] = f("L1_ffn_shared_w1").T
    w["sw2"] = f("L1_ffn_shared_w2").T.reshape(CH1, P, P).transpose(1, 0, 2).reshape(P, -1)
    w["ew1"] = f("L1_ffn_experts_w1").transpose(2, 0, 1).reshape(P, -1)
    w["ew2"] = f("L1_ffn_experts_w2").reshape(E1, P, CH1, P).transpose(3, 0, 2, 1).reshape(P, -1)
    return {n: c(v) for n, v in w.items()}


def kernel(**inputs):
    import concourse.bacc as bacc
    from concourse.bass_utils import run_bass_kernel_spmd

    nc = bacc.Bacc("TRN2", target_bir_lowering=False, num_devices=1)
    arrays = laid_out(inputs)
    aps = {n: nc.dram_tensor("in_" + n, v.shape, mybir.dt.from_np(v.dtype), kind="ExternalInput").ap()
           for n, v in arrays.items()}
    out = nc.dram_tensor("result", (NB, T, P), F32, kind="ExternalOutput").ap()
    build(nc, aps, out)
    return run_bass_kernel_spmd(nc, [{"in_" + n: v for n, v in arrays.items()}], core_ids=[0]).results[0]["result"]
```
